# Optimizing a Trainium2 kernel written in Bass

```python
import numpy as np
import jax
import jax.numpy as jnp

def _softmax(x, axis=-1):
    return jax.nn.softmax(x, axis=axis)

def _gelu(x):
    return jax.nn.gelu(x, approximate=True)

def _silu(x):
    return jax.nn.silu(x)

def _sigmoid(x):
    return jax.nn.sigmoid(x)

def _layernorm(x, axis=-1, eps=1e-05):
    m = jnp.mean(x, axis=axis, keepdims=True)
    v = jnp.var(x, axis=axis, keepdims=True)
    return (x - m) / jnp.sqrt(v + eps)

def _scatter_add(tgt, idx, src, axis=0):
    return tgt.at[idx].add(src)

def _segment_sum(src, seg, n):
    return jax.ops.segment_sum(src, seg, n)
kernel_name = 'mk_gnn_resnorm_d2_gnn_r32_dec835'

def setup_inputs(seed: int=0):
    np.random.seed(seed)
    _w = jnp.asarray

    def _rec_inputs():
        import jax
        import jax.numpy as jnp
        _gk = jax.random.key(seed)
        x = -0.000202 + 1 * jax.random.normal(jax.random.fold_in(_gk, 1), (3125, 64), jnp.float32)
        src = jax.random.randint(jax.random.fold_in(_gk, 2), (100000,), 0, 3125, jnp.int32)
        dst = jax.random.randint(jax.random.fold_in(_gk, 3), (100000,), 0, 3125, jnp.int32)
        _o = jnp.argsort(dst, stable=True)
        src = src[_o]
        dst = dst[_o]
        edge_attr_16 = -0.00010739 + 0.99994 * jax.random.normal(jax.random.fold_in(_gk, 12), (100000, 16), jnp.float32)
        edge_attr_32 = -8.62073e-06 + 0.999901 * jax.random.normal(jax.random.fold_in(_gk, 13), (100000, 32), jnp.float32)
        edge_type_3 = jax.random.randint(jax.random.fold_in(_gk, 14), (100000,), 0, 3, jnp.int32)
        node_type_2 = jax.random.randint(jax.random.fold_in(_gk, 15), (3125,), 0, 2, jnp.int32)
        return (x, src, dst, edge_attr_16, edge_attr_32, edge_type_3, node_type_2)
    x, src, dst, edge_attr_16, edge_attr_32, edge_type_3, node_type_2 = _rec_inputs()

    def _L0_gnn_setup():
        import jax, jax.numpy as jnp
        import numpy as np
        N, M = (3125, 25000)
        F_IN, F_E, H = (64, 16, 64)
        T_NODE, T_EDGE = (2, 3)
        HEAD_DIM = 16.0

        def _node_proj(x, W, b, node_type):
            p = jnp.einsum('nf,tfh->tnh', x, W) + b[:, None, :]
            return jnp.take_along_axis(p, node_type[None, :, None], axis=0)[0]
        key = jax.random.key(seed)
        ks = jax.random.split(key, 16)
        inp = {'x': jax.random.normal(ks[0], (N, F_IN), jnp.float32), 'edge_feat': jax.random.normal(ks[1], (M, F_E), jnp.float32), 'node_type': jax.random.randint(ks[2], (N,), 0, T_NODE, jnp.int32), 'edge_src': jax.random.randint(ks[3], (M,), 0, N, jnp.int32), 'edge_dst': jax.random.randint(ks[4], (M,), 0, N, jnp.int32), 'edge_type': jax.random.randint(ks[5], (M,), 0, T_EDGE, jnp.int32)}
        s_n = 1.0 / np.sqrt(F_IN)
        s_e = 1.0 / np.sqrt(F_E)
        for i, name in enumerate(['W1', 'W2', 'W3', 'W4']):
            inp[name] = jax.random.normal(ks[6 + i], (T_NODE, F_IN, H), jnp.float32) * s_n
            inp['b' + name[1]] = jax.random.normal(ks[10 + i], (T_NODE, H), jnp.float32) * 0.01
        inp['W5'] = jax.random.normal(ks[14], (T_EDGE, F_E, H), jnp.float32) * s_e
        inp['b5'] = jax.random.normal(ks[15], (T_EDGE, H), jnp.float32) * 0.01
        return inp
    _L0_gnn_all = _L0_gnn_setup()
    _L0_gnn_in = {k: v for k, v in _L0_gnn_all.items() if k in ('W1', 'b1', 'W2', 'b2', 'W3', 'b3', 'W4', 'b4', 'W5', 'b5')}
    del _L0_gnn_all

    def _L1_gnn_setup():
        import jax, jax.numpy as jnp
        import numpy as np
        N_NODES = 3125
        N_EDGES = 31250
        D_NODE = 64
        D_EDGE = 32
        D_OUT = 64
        EPS = 1e-07
        BETA = 1.0
        key = jax.random.key(seed)
        ks = jax.random.split(key, 6)
        node_feats = jax.random.normal(ks[0], (N_NODES, D_NODE), dtype=jnp.float32)
        edge_feats = jax.random.normal(ks[1], (N_EDGES, D_EDGE), dtype=jnp.float32)
        src = jax.random.randint(ks[2], (N_EDGES,), 0, N_NODES, dtype=jnp.int32)
        dst = jax.random.randint(ks[3], (N_EDGES,), 0, N_NODES, dtype=jnp.int32)
        We = jax.random.normal(ks[4], (D_EDGE, D_OUT), dtype=jnp.float32) / np.sqrt(D_EDGE)
        be = jnp.zeros((D_OUT,), dtype=jnp.float32)
        Wm = jax.random.normal(ks[5], (D_NODE, D_OUT), dtype=jnp.float32) / np.sqrt(D_NODE)
        bm = jnp.zeros((D_OUT,), dtype=jnp.float32)
        return {'node_feats': node_feats, 'edge_feats': edge_feats, 'src': src, 'dst': dst, 'We': We, 'be': be, 'Wm': Wm, 'bm': bm}
    _L1_gnn_all = _L1_gnn_setup()
    _L1_gnn_in = {k: v for k, v in _L1_gnn_all.items() if k in ('We', 'be', 'Wm', 'bm')}
    del _L1_gnn_all
    return {'x': x, 'src': src, 'dst': dst, 'edge_attr_16': edge_attr_16, 'edge_attr_32': edge_attr_32, 'edge_type_3': edge_type_3, 'node_type_2': node_type_2, 'L0_gnn_W1': _L0_gnn_in['W1'], 'L0_gnn_b1': _L0_gnn_in['b1'], 'L0_gnn_W2': _L0_gnn_in['W2'], 'L0_gnn_b2': _L0_gnn_in['b2'], 'L0_gnn_W3': _L0_gnn_in['W3'], 'L0_gnn_b3': _L0_gnn_in['b3'], 'L0_gnn_W4': _L0_gnn_in['W4'], 'L0_gnn_b4': _L0_gnn_in['b4'], 'L0_gnn_W5': _L0_gnn_in['W5'], 'L0_gnn_b5': _L0_gnn_in['b5'], 'L1_gnn_We': _L1_gnn_in['We'], 'L1_gnn_be': _L1_gnn_in['be'], 'L1_gnn_Wm': _L1_gnn_in['Wm'], 'L1_gnn_bm': _L1_gnn_in['bm']}

def reference(x, src, dst, edge_attr_16, edge_attr_32, edge_type_3, node_type_2, L0_gnn_W1, L0_gnn_b1, L0_gnn_W2, L0_gnn_b2, L0_gnn_W3, L0_gnn_b3, L0_gnn_W4, L0_gnn_b4, L0_gnn_W5, L0_gnn_b5, L1_gnn_We, L1_gnn_be, L1_gnn_Wm, L1_gnn_bm):
    import jax
    import jax.numpy as jnp

    def _L0_gnn_ref(x, edge_feat, W1, b1, W2, b2, W3, b3, W4, b4, W5, b5, node_type, edge_src, edge_dst, edge_type):
        import jax, jax.numpy as jnp
        import numpy as np
        N, M = (3125, 25000)
        F_IN, F_E, H = (64, 16, 64)
        T_NODE, T_EDGE = (2, 3)
        HEAD_DIM = 16.0

        def _node_proj(x, W, b, node_type):
            p = jnp.einsum('nf,tfh->tnh', x, W) + b[:, None, :]
            return jnp.take_along_axis(p, node_type[None, :, None], axis=0)[0]
        n = x.shape[0]
        h1 = _node_proj(x, W1, b1, node_type)
        h2 = _node_proj(x, W2, b2, node_type)
        h3 = _node_proj(x, W3, b3, node_type)
        h4 = _node_proj(x, W4, b4, node_type)
        w5e = jnp.einsum('mf,mfh->mh', edge_feat, W5[edge_type]) + b5[edge_type]
        num = jnp.sum(h3[edge_dst] * (h4[edge_src] + w5e), axis=-1)
        score = jax.nn.softmax((num / jnp.sqrt(HEAD_DIM))[:, None], axis=-1)[:, 0]
        msg = score[:, None] * (h2[edge_src] + w5e)
        out = h1 + jax.ops.segment_sum(msg, edge_dst, num_segments=n)
        return out

    def _L1_gnn_ref(node_feats, edge_feats, src, dst, We, be, Wm, bm):
        import jax, jax.numpy as jnp
        import numpy as np
        N_NODES = 3125
        N_EDGES = 31250
        D_NODE = 64
        D_EDGE = 32
        D_OUT = 64
        EPS = 1e-07
        BETA = 1.0
        n = node_feats.shape[0]
        m = node_feats[src] + (edge_feats @ We + be)
        m = jax.nn.relu(m) + EPS
        z = m * BETA
        zmax = jax.ops.segment_max(z, dst, num_segments=n)
        ez = jnp.exp(z - zmax[dst])
        denom = jax.ops.segment_sum(ez, dst, num_segments=n)
        a = ez / denom[dst]
        agg = jax.ops.segment_sum(m * a, dst, num_segments=n)
        feats = node_feats + agg
        return feats @ Wm + bm
    x = _layernorm(x + _L0_gnn_ref(x, edge_attr_16, L0_gnn_W1, L0_gnn_b1, L0_gnn_W2, L0_gnn_b2, L0_gnn_W3, L0_gnn_b3, L0_gnn_W4, L0_gnn_b4, L0_gnn_W5, L0_gnn_b5, node_type_2, src, dst, edge_type_3), axis=-1)
    x = _layernorm(x + _L1_gnn_ref(x, edge_attr_32, src, dst, L1_gnn_We, L1_gnn_be, L1_gnn_Wm, L1_gnn_bm), axis=-1)
    return x

_drawn_inputs = setup_inputs


def setup_inputs(seed=0):
    import zlib

    import numpy as np

    out = dict(_drawn_inputs(seed))
    spreads = {'L1_gnn_be': (0.0, 0.1), 'L1_gnn_bm': (0.0, 0.1)}
    factors = {'L0_gnn_b1': 53.308}
    for name, (base, spread) in spreads.items():
        noise = np.random.default_rng([zlib.crc32(name.encode()), seed]).standard_normal(out[name].shape)
        drawn = base * np.exp(spread * noise) if base else spread * noise
        out[name] = jnp.asarray(drawn.astype(out[name].dtype))
    for name, factor in factors.items():
        out[name] = (out[name] * factor).astype(out[name].dtype)
    return out
```

```python
import concourse.bass as bass
from concourse import mybir
from contextlib import ExitStack

N_NODES = 3125
N_EDGES = 100000
C = 64
F0, F1 = 16, 32
T_EDGE = 3
P = 128
NP = 125
NT = N_NODES // NP
CH = 512
TILES = CH // P
CHUNKS = 2 * -(-N_EDGES // (4 * CH))
HALF = CHUNKS * CH
EP = 2 * HALF
ROWS = EP // P
CUT_ROW = 2 * (HALF - 1)
DUMP = EP
EPS = 1e-7
LN_EPS = 1e-5
BIG = 1e30


def gnn_program(nc, t, out):
    f32, bf16, i32 = mybir.dt.float32, mybir.dt.bfloat16, mybir.dt.int32
    ALU, ACT, AX = mybir.AluOpType, mybir.ActivationFunctionType, mybir.AxisListType
    ctx = ExitStack()
    with ctx:
        def sb(name, shape, dt=f32):
            return ctx.enter_context(nc.sbuf_tensor(name, shape, dt))

        def pb(name, cols):
            return ctx.enter_context(nc.psum_tensor(name, [P, cols], f32))

        def sem(name):
            return ctx.enter_context(nc.semaphore(name))

        def sems(name):
            return [sem(f"{name}_{s}") for s in range(2)]

        def scratch(name, shape, dt=f32):
            return nc.dram_tensor(name, shape, dt).ap()

        d_keep = scratch("d_keep", [1, EP], bf16)
        d_pen = scratch("d_pen", [1, EP], bf16)
        d_type = scratch("d_type", [1, EP], bf16)
        d_h24 = scratch("d_h24", [N_NODES, 2 * C])
        d_h3 = scratch("d_h3", [N_NODES, C])
        d_inj = scratch("d_inj", [EP + NP * NT, C])
        d_run0 = scratch("d_run0", [EP, C])
        d_x1 = scratch("d_x1", [N_NODES, C])
        d_run1 = scratch("d_run1", [EP, 2 * C])
        d_max = scratch("d_max", [C * HALF, 1])

        ident = sb("ident", [P, P])
        half_ones = sb("half_ones", [P, P])
        type_of_row = sb("type_of_row", [P, 1])
        ones = sb("ones", [NP, C])
        zeros = sb("zeros", [P, 1792])
        w_nodes = sb("w_nodes", [C + 1, 2, 4 * C])
        w5 = sb("w5", [P, P])
        we = sb("we", [P, P])
        wm = sb("wm", [C + 1, C])
        xT = sb("xT", [C + 1, N_NODES])
        x_sb = sb("x_sb", [NP, NT, C])
        ntype_i = sb("ntype_i", [NP, NT], i32)
        is_type = sb("is_type", [NP, 2, NT])
        H = sb("H", [NP, NT, 4 * C])
        node_i = sb("node_i", [NP, NT], i32)
        node = sb("node", [NP, NT])
        keys = sb("keys", [NP, ROWS], i32)
        full_rows = sb("full_rows", [NP, NT])
        row_i = sb("row_i", [NP, NT], i32)
        found = sb("found", [NP, NT, P], i32)
        le = sb("le", [NP, NT, P], bf16)
        le_row = le[:, :, :].rearrange("p i k -> p (i k)")[:, 0:ROWS]
        in_row = sb("in_row", [NP, NT])
        end = sb("end", [NP, NT])
        start = sb("start", [NP, NT])
        has_edges = sb("has_edges", [NP, NT])
        last = sb("last", [NP, NT])
        last_i = sb("last_i", [NP, NT], i32)
        tmp_n = sb("tmp_n", [NP, NT])
        first_i = sb("first_i", [NP, NT], i32)
        mid_i = sb("mid_i", [NP, 2], i32)
        mid = sb("mid", [NP, 2])
        mid_same = sb("mid_same", [NP, 1])
        cross = sb("cross", [NP, NT])
        not_cross = sb("not_cross", [NP, NT])
        fix = sb("fix", [16, C])
        mb_col = sb("mb_col", [NP, 1])
        lane_i = sb("lane_i", [C, 1], i32)
        lane = sb("lane", [C, 1])
        mb_i = sb("mb_i", [C, 1], i32)
        max_ab = sb("max_ab", [C, 2])
        max_ab_wide = sb("max_ab_wide", [C, 2, NP])
        dst_i = sb("dst_i", [P, ROWS], i32)
        prev_i = sb("prev_i", [P, ROWS], i32)
        type_i = sb("type_i", [P, ROWS], i32)
        dst_step = sb("dst_step", [P, ROWS])
        keep_r = sb("keep_r", [P, ROWS], bf16)
        pen_r = sb("pen_r", [P, ROWS], bf16)
        type_r = sb("type_r", [P, ROWS], bf16)
        idx = [sb(f"idx{s}", [P, 2 * TILES], i32) for s in range(2)]
        rows0 = [sb(f"rows0_{s}", [P, TILES, 2, 2 * C]) for s in range(2)]
        rows1 = [r[:, :, :, :].rearrange("p j h c -> p (j h c)")[:, 0:TILES * 2 * C].rearrange("p (j h c) -> p j h c", j=TILES, h=2)
                 for r in rows0]
        types = [sb(f"types{s}", [P, CH], bf16) for s in range(2)]
        feat = [sb(f"feat{s}", [P, CH]) for s in range(2)]
        featm = [sb(f"featm{s}", [P, CH]) for s in range(2)]
        keep = [sb(f"keep{s}", [P, CH], bf16) for s in range(2)]
        inj = [sb(f"inj{s}", [P, TILES, 2 * C]) for s in range(2)]
        h3d = [sb(f"h3d{s}", [P, CH]) for s in range(2)]
        prod = [sb(f"prod{s}", [P, CH]) for s in range(2)]
        scor = [sb(f"scor{s}", [P, CH]) for s in range(2)]
        dif = [sb(f"dif{s}", [P, CH]) for s in range(2)]
        exps = [sb(f"exps{s}", [P, CH]) for s in range(2)]
        prob = [sb(f"prob{s}", [P, CH]) for s in range(2)]
        inv = scor
        msg = [sb(f"msg{s}", [P, CH]) for s in range(2)]
        run = [sb(f"run{s}", [P, CH]) for s in range(2)]
        stage0 = [sb(f"stage0_{s}", [P, TILES, 2 * C]) for s in range(2)]
        relu, m, y, up, down = prod, h3d, scor, dif, exps
        decay, expm, mexp = prob, msg, run
        runmax = [sb(f"runmax{s}", [P, CH + 1]) for s in range(2)]
        run_s = [sb(f"run_s{s}", [P, CH]) for s in range(2)]
        run_n = [sb(f"run_n{s}", [P, CH]) for s in range(2)]
        stage1 = [sb(f"stage1_{s}", [P, TILES, 2, 2, C]) for s in range(2)]
        got0 = sb("got0", [NP, NT, C])
        cut0 = sb("cut0", [NP, C])
        acc = sb("acc", [NP, NT, C])
        x1 = sb("x1", [NP, NT, C])
        sq = sb("sq", [NP, NT, C])
        mean = sb("mean", [NP, NT])
        var = sb("var", [NP, NT])
        std = sb("std", [NP, NT])
        rstd = sb("rstd", [NP, NT])
        got1 = H[:, :, 0:2 * C].rearrange("p i (q c) -> p i q c", q=2)
        cut1 = sb("cut1", [NP, 2, C])
        mx = sb("mx", [NP, 2, C])
        mm = sb("mm", [NP, C])
        dmx = sb("dmx", [NP, 2, C])
        wgt = sb("wgt", [NP, 2, C])
        scale_b = found[:, :, 0:C].bitcast(f32)
        featsT = [sb(f"featsT{s}", [C + 1, NP]) for s in range(2)]
        y_out = found[:, :, C:2 * C].bitcast(f32)

        wide = [pb(f"wide{s}", 2 * CH) for s in range(2)]
        bank = [pb(f"bank{b}", CH) for b in range(4)]
        q2 = [w[:, 0:CH] for w in wide]
        q4 = [w[:, CH:2 * CH] for w in wide]
        p_inj, p_num, p_out0 = bank[0:2], bank[2], bank[3]
        p_m, p_out1 = bank[0:2], wide

        s_const, s_nodes, s_edges = sem("s_const"), sem("s_nodes"), sem("s_edges")
        s_wzero, s_weights, s_ones = sem("s_wzero"), sem("s_weights"), sem("s_ones")
        s_keys, s_iota, s_zeros = sem("s_keys"), sem("s_iota"), sem("s_zeros")
        s_istype, s_proj, s_proj0, s_sel = sem("s_istype"), sem("s_proj"), sem("s_proj0"), sem("s_sel")
        s_h24, s_h3, s_rowlists, s_lists = sem("s_h24"), sem("s_h3"), sem("s_rowlists"), sem("s_lists")
        s_row_i, s_found, s_end, s_shift = sem("s_row_i"), sem("s_found"), sem("s_end"), sem("s_shift")
        s_start0 = sem("s_start0")
        s_first_i, s_last_i, s_injzero, s_inj = sem("s_first_i"), sem("s_last_i"), sem("s_injzero"), sem("s_inj")
        s_fix, s_fixed, s_mbcol, s_mbps, s_mb_i = sem("s_fix"), sem("s_fixed"), sem("s_mbcol"), sem("s_mbps"), sem("s_mb_i")
        s_vec = sem("s_vec")
        s_chunks = sem("s_chunks")
        s_init = sem("s_init")
        idx_in, got_rows, feat_in, keep_in, inj_in = sems("idx_in"), sems("got_rows"), sems("feat_in"), sems("keep_in"), sems("inj_in")
        masked, q4_ready, q2_ready, injT = sems("masked"), sems("q4_ready"), sems("q2_ready"), sems("injT")
        h3_ready, prod_ready, num_ready, scor_ready = sems("h3_ready"), sems("prod_ready"), sems("num_ready"), sems("scor_ready")
        dif_ready, exps_ready, inv_ready, prob_ready, msg_ready = (sems("dif_ready"), sems("exps_ready"), sems("inv_ready"),
                                                                   sems("prob_ready"), sems("msg_ready"))
        run_ready, runT, staged, stored = sems("run_ready"), sems("runT"), sems("staged"), sems("stored")
        s_cut0, s_got0, s_acc0, s_sqrt, s_x1, s_x1_out = sem("s_cut0"), sem("s_got0"), sem("s_acc0"), sem("s_sqrt"), sem("s_x1"), sem("s_x1_out")
        idx1_in, got1_rows, feat1_in, pen_in = sems("idx1_in"), sems("got1_rows"), sems("feat1_in"), sems("pen_in")
        z_ready, relu_ready, m_ready = sems("z_ready"), sems("relu_ready"), sems("m_ready")
        carry_ready, max_ready, shift_ready, y_ready = sems("carry_ready"), sems("max_ready"), sems("shift_ready"), sems("y_ready")
        updown_ready, decay_ready, expm_ready = sems("updown_ready"), sems("decay_ready"), sems("expm_ready")
        mexp_ready, s_run, n_run, run1T, staged1, stored1, max_out = (sems("mexp_ready"), sems("s_run"), sems("n_run"),
                                                                     sems("run1T"), sems("staged1"), sems("stored1"), sems("max_out"))
        s_ones1 = sem("s_ones1")
        s_cut1, s_got1, s_mb, s_maxwide, s_maxps, s_dmx, s_wgt = (sem("s_cut1"), sem("s_got1"), sem("s_mb"), sem("s_maxwide"),
                                                                  sem("s_maxps"), sem("s_dmx"), sem("s_wgt"))
        s_feats, s_fT, s_fTsb, s_y, s_ysum, s_fin, s_out = (sem("s_feats"), sem("s_fT"), sem("s_fTsb"), sem("s_y"),
                                                           sem("s_ysum"), sem("s_fin"), sem("s_out"))

        LOADS_CONST, LOADS_W = 3, 20
        block = ctx.enter_context(nc.Block())

        def at(i, k):
            return k % 2, i + k // 2

        @block.sync
        def _(sp):
            sp.dma_start(keys[:, :], t["keys"].to_broadcast([NP, ROWS])).then_inc(s_keys, 16)
            sp.dma_start(mid_i[:, :], t["mid"].to_broadcast([NP, 2])).then_inc(s_keys, 16)
            sp.dma_start(xT[0:C, :], t["xT"]).then_inc(s_nodes, 16)
            sp.dma_start(ntype_i[:, :], t["node_type"]).then_inc(s_nodes, 16)
            for name, a, b in (("1", 0, C), ("24", C, 3 * C), ("3", 3 * C, 4 * C)):
                sp.dma_start(w_nodes[0:C, :, a:b], t["W" + name].rearrange("t f h -> f t h")).then_inc(s_nodes, 16)
                sp.dma_start(w_nodes[C:C + 1, :, a:b], t["b" + name].rearrange("(a t) h -> a t h", a=1)).then_inc(s_nodes, 16)
            sp.dma_start(dst_i[:, :], t["dst"].rearrange("a b -> (a b)").rearrange("(p k) -> p k", p=P)).then_inc(s_edges, 16)
            sp.dma_start(prev_i[:, :], t["dst_prev"]).then_inc(s_edges, 16)
            sp.dma_start(type_i[:, :], t["etype"]).then_inc(s_edges, 16)
            sp.dma_start(ident[:, :], t["ident"]).then_inc(s_const, 16)
            sp.dma_start(half_ones[:, :], t["half_ones"]).then_inc(s_const, 16)
            sp.dma_start(type_of_row[:, :], t["type_of_row"]).then_inc(s_const, 16)
            sp.dma_start(x_sb[:, :, :], t["x"].rearrange("(p i) c -> p i c", i=NT)).then_inc(s_const, 16)
            sp.wait_ge(s_wzero, 2)
            for h in range(2):
                b = h * C
                sp.dma_start(w5[b:b + T_EDGE * F0, b:b + C], t["W5"].rearrange("t f h -> (t f) h")).then_inc(s_weights, 16)
                sp.dma_start(w5[b + T_EDGE * F0:b + T_EDGE * (F0 + 1), b:b + C], t["b5"]).then_inc(s_weights, 16)
                sp.dma_start(we[b:b + F1, b:b + C], t["We"]).then_inc(s_weights, 16)
                sp.dma_start(we[b + F1:b + F1 + 1, b:b + C], t["be"]).then_inc(s_weights, 16)
            sp.dma_start(wm[0:C, :], t["Wm"]).then_inc(s_weights, 16)
            sp.dma_start(wm[C:C + 1, :], t["bm"]).then_inc(s_weights, 16)
            sp.wait_ge(s_rowlists, 3)
            for dst, src in ((d_keep, keep_r), (d_pen, pen_r), (d_type, type_r)):
                sp.dma_start(dst.rearrange("a (p b) -> (a p) b", p=P), src[:, :]).then_inc(s_lists, 16)
            sp.wait_ge(s_end, 1)
            sp.wait_ge(s_start0, 1)
            sp.dma_start(start[1:NP, 0:1], end[0:NP - 1, NT - 1:NT]).then_inc(s_shift, 16)
            sp.wait_ge(s_sel, NT)
            sp.dma_start(d_h24.rearrange("(p i) c -> p i c", i=NT), H[:, :, C:3 * C]).then_inc(s_h24, 16)
            sp.dma_start(d_h3.rearrange("(p i) c -> p i c", i=NT), H[:, :, 3 * C:4 * C]).then_inc(s_h3, 16)
            sp.wait_ge(s_fix, 16)
            sp.wait_ge(s_inj, 16 * NT)
            sp.dma_start(d_inj[1:2, :], fix[0:1, :]).then_inc(s_fixed, 16)

            sp.wait_ge(s_lists, 48)
            sp.wait_ge(s_ones, 1)

            def load_chunk0(i, s, c):
                of_src, of_inj = sp.snap(c * P), sp.snap(c * (2 * CH))
                of_edge = [sp.snap(c * CH), sp.snap(c * CH + HALF)]
                sp.wait_ge(got_rows[s], 16 * 2 * TILES * i)
                sp.dma_start(idx[s][:, :], t["src"][bass.ds(of_src, P), :]).then_inc(idx_in[s], 16)
                sp.wait_ge(masked[s], i)
                for h in range(2):
                    sp.dma_start(types[s][h * C:(h + 1) * C, :],
                                 d_type[:, bass.ds(of_edge[h], CH)].to_broadcast([C, CH])).then_inc(feat_in[s], 16)
                    for k in range(T_EDGE):
                        sp.dma_start(feat[s][h * C + k * F0:h * C + (k + 1) * F0, :],
                                     t["ea16T"][:, bass.ds(of_edge[h], CH)]).then_inc(feat_in[s], 16)
                sp.wait_ge(injT[s], i)
                sp.dma_start(inj[s][:, :, :], d_inj[bass.ds(of_inj, 2 * CH), :]
                             .rearrange("(p j h) c -> p j (h c)", j=TILES, h=2)).then_inc(inj_in[s], 16)
                sp.wait_ge(run_ready[s], i)
                for h in range(2):
                    sp.dma_start(keep[s][h * C:(h + 1) * C, :],
                                 d_keep[:, bass.ds(of_edge[h], CH)].to_broadcast([C, CH])).then_inc(keep_in[s], 16)

            sp.wait_ge(s_fixed, 16)
            with sp.Fori(0, CHUNKS // 2) as i:
                for s in range(2):
                    load_chunk0(i, s, 2 * i + s)

            for s in range(2):
                sp.wait_ge(stored[s], 16 * (CHUNKS // 2))
            sp.dma_start(cut0[:, :], d_run0[CUT_ROW:CUT_ROW + 1, :].to_broadcast([NP, C])).then_inc(s_cut0, 16)
            sp.wait_ge(s_x1, 1)
            sp.dma_start(d_x1.rearrange("(p i) c -> p i c", i=NT), x1[:, :, :]).then_inc(s_x1_out, 16)
            sp.wait_ge(s_ones1, 1)

            with sp.Fori(0, CHUNKS // 2) as i:
                for s in range(2):
                    c = 2 * i + s
                    of_src, of_edge = sp.snap(c * P), [sp.snap(c * CH), sp.snap(c * CH + HALF)]
                    sp.wait_ge(got1_rows[s], 16 * 2 * TILES * i)
                    sp.dma_start(idx[s][:, :], t["src"][bass.ds(of_src, P), :]).then_inc(idx1_in[s], 16)
                    sp.wait_ge(z_ready[s], i)
                    for h in range(2):
                        sp.dma_start(feat[s][h * C:h * C + F1, :],
                                     t["ea32T"][:, bass.ds(of_edge[h], CH)]).then_inc(feat1_in[s], 16)
                    sp.wait_ge(s_lists, 48)
                    sp.wait_ge(shift_ready[s], i)
                    for h in range(2):
                        sp.dma_start(keep[s][h * C:(h + 1) * C, :],
                                     d_pen[:, bass.ds(of_edge[h], CH)].to_broadcast([C, CH])).then_inc(pen_in[s], 16)

            for s in range(2):
                sp.wait_ge(stored1[s], 16 * (CHUNKS // 2))
            sp.dma_start(cut1[:, :, :], d_run1[CUT_ROW:CUT_ROW + 1, :].rearrange("a (q c) -> a q c", q=2).to_broadcast([NP, 2, C])).then_inc(s_cut1, 16)
            sp.wait_ge(s_fin, 1)
            sp.dma_start(out.rearrange("(p i) c -> p i c", i=NT), x1[:, :, :]).then_inc(s_out, 16)
            sp.wait_ge(s_out, 16)

        @block.gpsimd
        def _(pool):
            pool.iota(node_i[:, :], pattern=[[1, NT]], base=0, channel_multiplier=NT).then_inc(s_iota, 1)
            pool.iota(lane_i[:, :], pattern=[[0, 1]], base=0, channel_multiplier=HALF).then_inc(s_iota, 1)
            pool.wait_ge(s_row_i, 1)
            for i in range(NT):
                pool.indirect_dma_start(out=found[:, i, :], out_offset=None, in_=t["dst"],
                                        in_offset=bass.IndirectOffsetOnAxis(ap=row_i[:, i:i + 1], axis=0)).then_inc(s_found, 16)
            pool.wait_ge(s_h3, 16)
            pool.indirect_dma_start(out=fix[:, :], out_offset=None, in_=d_h3,
                                    in_offset=bass.IndirectOffsetOnAxis(ap=mid_i[0:16, 1:2], axis=0)).then_inc(s_fix, 16)
            pool.wait_ge(s_injzero, 16 * 28)
            pool.wait_ge(s_first_i, 1)
            for i in range(NT):
                pool.indirect_dma_start(out=d_inj, out_offset=bass.IndirectOffsetOnAxis(ap=first_i[:, i:i + 1], axis=0),
                                        in_=H[:, i, 3 * C:4 * C], in_offset=None).then_inc(s_inj, 16)
            with pool.Fori(0, CHUNKS // 2) as i:
                for s in range(2):
                    pool.wait_ge(s_h24, 16)
                    pool.wait_ge(idx_in[s], 16 * (i + 1))
                    pool.wait_ge(q2_ready[s], i)
                    pool.sem_inc(s_chunks, 1)
                    for j in range(2 * TILES):
                        pool.indirect_dma_start(out=rows0[s][:, j % TILES, j // TILES, :], out_offset=None, in_=d_h24,
                                                in_offset=bass.IndirectOffsetOnAxis(ap=idx[s][:, j:j + 1], axis=0)).then_inc(got_rows[s], 16)
            pool.wait_ge(s_last_i, 1)
            for s in range(2):
                pool.wait_ge(stored[s], 16 * (CHUNKS // 2))
            for i in range(NT):
                pool.indirect_dma_start(out=got0[:, i, :], out_offset=None, in_=d_run0,
                                        in_offset=bass.IndirectOffsetOnAxis(ap=last_i[:, i:i + 1], axis=0)).then_inc(s_got0, 16)
            with pool.Fori(0, CHUNKS // 2) as i:
                for s in range(2):
                    pool.wait_ge(s_x1_out, 16)
                    pool.wait_ge(idx1_in[s], 16 * (i + 1))
                    pool.wait_ge(z_ready[s], i)
                    pool.sem_inc(s_chunks, 1)
                    for j in range(2 * TILES):
                        pool.indirect_dma_start(out=rows1[s][:, j % TILES, j // TILES, :], out_offset=None, in_=d_x1,
                                                in_offset=bass.IndirectOffsetOnAxis(ap=idx[s][:, j:j + 1], axis=0)).then_inc(got1_rows[s], 16)
            pool.wait_ge(s_mb_i, 1)
            for s in range(2):
                pool.wait_ge(max_out[s], 16 * (CHUNKS // 2))
            pool.indirect_dma_start(out=max_ab[:, 1:2], out_offset=None, in_=d_max,
                                    in_offset=bass.IndirectOffsetOnAxis(ap=mb_i[:, 0:1], axis=0)).then_inc(s_mb, 16)
            for s in range(2):
                pool.wait_ge(stored1[s], 16 * (CHUNKS // 2))
            for i in range(NT):
                pool.indirect_dma_start(out=H[:, i, 0:2 * C], out_offset=None, in_=d_run1,
                                        in_offset=bass.IndirectOffsetOnAxis(ap=last_i[:, i:i + 1], axis=0)).then_inc(s_got1, 16)

        @block.scalar
        def _(act):
            act.wait_ge(s_zeros, 1)
            flat = d_inj[0:EP, :].rearrange("(z p r) c -> z p (r c)", z=28, p=P)
            for z in range(28):
                act.dma_start(flat[z], zeros[:, :]).then_inc(s_injzero, 16)
            act.wait_ge(s_istype, 2)
            for i in range(NT):
                act.wait_ge(s_proj, i + 1)
                act.activation(H[:, i, :], bank[i % 2][0:NP, 0:4 * C], ACT.Copy, scale=is_type[:, 0, i:i + 1]).then_inc(s_proj0, 1)

            def scores(s, r):
                act.wait_ge(num_ready[s], r + 1)
                act.wait_ge(prob_ready[s], r)
                act.activation(scor[s][:, :], p_num[:, :], ACT.Copy, scale=0.25).then_inc(scor_ready[s], 1)

            def exponents(s, r):
                act.wait_ge(dif_ready[s], r + 1)
                act.activation(exps[s][:, :], dif[s][:, :], ACT.Exp).then_inc(exps_ready[s], 1)

            def store0(s, r, c):
                act.wait_ge(runT[s], r + 1)
                act.wait_ge(stored[s], 16 * r)
                act.activation(stage0[s][:, :, :].rearrange("p j c -> p (j c)"), p_out0[:, :], ACT.Copy).then_inc(staged[s], 1)
                act.wait_ge(staged[s], r + 1)
                act.dma_start(d_run0[bass.ds(2 * CH * c, 2 * CH), :].rearrange("(p j h) c -> p j (h c)", j=TILES, h=2),
                              stage0[s][:, :, :]).then_inc(stored[s], 16)

            scores(0, 0)
            with act.Fori(0, CHUNKS // 2 - 1) as i:
                for k in (1, 2):
                    exponents(*at(i, k - 1))
                    scores(*at(i, k))
                    store0(*at(i, k - 1), 2 * i + k - 1)
            LAST = CHUNKS // 2 - 1
            exponents(0, LAST)
            scores(1, LAST)
            store0(0, LAST, CHUNKS - 2)
            exponents(1, LAST)
            store0(1, LAST, CHUNKS - 1)

            act.wait_ge(s_acc0, 1)
            act.activation(std[:, :], var[:, :], ACT.Sqrt).then_inc(s_sqrt, 1)

            def messages(s, r):
                act.wait_ge(z_ready[s], r + 1)
                act.activation(relu[s][:, :], p_m[s][:, :], ACT.Relu).then_inc(relu_ready[s], 1)
                act.wait_ge(relu_ready[s], r + 1)
                act.wait_ge(mexp_ready[s], r)
                act.activation(m[s][:, :], relu[s][:, :], ACT.Copy, bias=EPS).then_inc(m_ready[s], 1)

            def decays(s, r):
                act.wait_ge(y_ready[s], r + 1)
                act.activation(up[s][:, :], y[s][:, :], ACT.Relu).then_inc(updown_ready[s], 1)
                act.activation(down[s][:, :], y[s][:, :], ACT.Relu, scale=-1.0).then_inc(updown_ready[s], 1)
                act.wait_ge(n_run[s], r)
                act.wait_ge(updown_ready[s], 2 * r + 2)
                act.activation(expm[s][:, :], down[s][:, :], ACT.Exp, scale=-1.0).then_inc(expm_ready[s], 1)
                act.activation(decay[s][:, :], up[s][:, :], ACT.Exp, scale=-1.0).then_inc(decay_ready[s], 1)

            def store1(s, r, c):
                act.wait_ge(run1T[s], r + 1)
                act.wait_ge(stored1[s], 16 * r)
                turned = p_out1[s][:, :].rearrange("p (j q h c) -> p j q h c", j=TILES, q=2, h=2)
                for q in range(2):
                    act.activation(stage1[s][:, :, :, q, :], turned[:, :, q], ACT.Copy).then_inc(staged1[s], 1)
                act.wait_ge(staged1[s], 2 * r + 2)
                act.dma_start(d_run1[bass.ds(2 * CH * c, 2 * CH), :].rearrange("(p j h) c -> p (j h c)", j=TILES, h=2),
                              stage1[s][:, :, :, :, :].rearrange("p j h q c -> p (j h q c)")).then_inc(stored1[s], 16)

            def store_max(s, r, c):
                act.dma_start(d_max.rearrange("(c e) a -> c (e a)", c=C)[:, bass.ds(c * CH, CH)],
                              runmax[s][C:P, 1:CH + 1]).then_inc(max_out[s], 16)

            messages(0, 0)
            decays(0, 0)
            store_max(0, 0, 0)
            messages(1, 0)
            with act.Fori(0, CHUNKS // 2 - 1) as i:
                for k in (1, 2):
                    decays(*at(i, k))
                    store_max(*at(i, k), 2 * i + k)
                    messages(*at(i, k + 1))
                    store1(*at(i, k - 1), 2 * i + k - 1)
            decays(1, LAST)
            store_max(1, LAST, CHUNKS - 1)
            store1(0, LAST, CHUNKS - 2)
            store1(1, LAST, CHUNKS - 1)

            act.wait_ge(s_dmx, 1)
            act.activation(wgt[:, :, :], dmx[:, :, :], ACT.Exp).then_inc(s_wgt, 1)
            for i in range(NT):
                act.wait_ge(s_fT, i + 1)
                if i >= 2:
                    act.wait_ge(s_y, i - 1)
                act.activation(featsT[i % 2][0:C, :], bank[i % 2][0:C, 0:NP], ACT.Copy).then_inc(s_fTsb, 1)
            act.wait_ge(s_acc0, 2)
            act.activation(std[:, :], var[:, :], ACT.Sqrt).then_inc(s_sqrt, 1)

        @block.tensor
        def _(pe):
            pe.wait_ge(s_nodes, 16 * 8)
            pe.wait_ge(s_init, 1)
            for i in range(NT):
                if i >= 2:
                    pe.wait_ge(s_sel, i - 1)
                pe.matmul(bank[i % 2][0:NP, :], xT[:, i:N_NODES:NT], w_nodes[:, :, :].rearrange("k t h -> k (t h)"),
                          start=True, stop=True).then_inc(s_proj, 1)
            pe.wait_ge(s_mbcol, 1)
            pe.wait_ge(s_sel, NT)
            pe.matmul(bank[2][0:C, 0:1], ones[:, :], mb_col[:, :], start=True, stop=True).then_inc(s_mbps, 1)
            pe.wait_ge(s_const, 16 * 4)
            pe.wait_ge(s_weights, 16 * 10)
            pe.wait_ge(s_mb_i, 1)

            def project0(s, r):
                pe.wait_ge(masked[s], r + 1)
                pe.wait_ge(prod_ready[s], r)
                pe.matmul(q4[s], w5[:, :], featm[s][:, :], start=True, stop=True)
                pe.wait_ge(got_rows[s], 16 * 2 * TILES * (r + 1))
                for j in range(TILES):
                    ins = pe.matmul(q4[s][:, j:CH:TILES], rows0[s][:, j, :, :].rearrange("p h c -> p (h c)")[:, 1:4 * C:2], ident[:, :],
                                    start=False, stop=True, skip_group_check=True)
                ins.then_inc(q4_ready[s], 1)
                pe.wait_ge(inj_in[s], 16 * (r + 1))
                pe.wait_ge(h3_ready[s], r)
                for j in range(TILES):
                    ins = pe.matmul(p_inj[s][:, j:CH:TILES], inj[s][:, j, :], ident[:, :], is_transpose=True,
                                    start=True, stop=True)
                ins.then_inc(injT[s], 1)
                pe.wait_ge(msg_ready[s], r)
                pe.matmul(q2[s], w5[:, :], featm[s][:, :], start=True, stop=True)
                for j in range(TILES):
                    ins = pe.matmul(q2[s][:, j:CH:TILES], rows0[s][:, j, :, :].rearrange("p h c -> p (h c)")[:, 0:4 * C:2], ident[:, :],
                                    start=False, stop=True, skip_group_check=True)
                ins.then_inc(q2_ready[s], 1)

            def numerator(s, r, s_prev, r_prev):
                pe.wait_ge(prod_ready[s], r + 1)
                if r_prev is not None:
                    pe.wait_ge(scor_ready[s_prev], r_prev + 1)
                pe.matmul(p_num[:, :], half_ones[:, :], prod[s][:, :], start=True, stop=True).then_inc(num_ready[s], 1)

            def turn0(s, r, s_prev, r_prev):
                pe.wait_ge(run_ready[s], r + 1)
                if r_prev is not None:
                    pe.wait_ge(staged[s_prev], r_prev + 1)
                for j in range(TILES):
                    ins = pe.matmul(p_out0[:, j * P:(j + 1) * P], run[s][:, j:CH:TILES], ident[:, :], is_transpose=True,
                                    start=True, stop=True)
                ins.then_inc(runT[s], 1)

            LAST = CHUNKS // 2 - 1
            project0(0, 0)
            numerator(0, 0, 0, None)
            project0(1, 0)
            numerator(1, 0, 0, 0)
            project0(0, 1)
            turn0(0, 0, 0, None)
            with pe.Fori(0, CHUNKS // 2 - 2) as i:
                for k in (2, 3):
                    numerator(*at(i, k), *at(i, k - 1))
                    project0(*at(i, k + 1))
                    turn0(*at(i, k - 1), *at(i, k - 2))
            numerator(0, LAST, 1, LAST - 1)
            project0(1, LAST)
            turn0(1, LAST - 1, 0, LAST - 1)
            numerator(1, LAST, 0, LAST)
            turn0(0, LAST, 1, LAST - 1)
            turn0(1, LAST, 0, LAST)

            def project1(s, r):
                pe.wait_ge(feat1_in[s], 32 * (r + 1))
                pe.wait_ge(relu_ready[s], r)
                pe.matmul(p_m[s][:, :], we[:, :], feat[s][:, :], start=True, stop=True)
                pe.wait_ge(got1_rows[s], 16 * 2 * TILES * (r + 1))
                for j in range(TILES):
                    ins = pe.matmul(p_m[s][:, j:CH:TILES], rows1[s][:, j, :, :].rearrange("p h c -> p (h c)"), ident[:, :],
                                    start=False, stop=True, skip_group_check=True)
                ins.then_inc(z_ready[s], 1)

            def turn1(s, r):
                pe.wait_ge(n_run[s], r + 1)
                pe.wait_ge(staged1[s], 2 * r)
                for j in range(TILES):
                    for q, src in enumerate((run_s[s], run_n[s])):
                        ins = pe.matmul(p_out1[s][:, (2 * j + q) * P:(2 * j + q + 1) * P], src[:, j:CH:TILES], ident[:, :],
                                        is_transpose=True, start=True, stop=True)
                ins.then_inc(run1T[s], 1)

            project1(0, 0)
            project1(1, 0)
            with pe.Fori(0, CHUNKS // 2 - 1) as i:
                for k in (1, 2):
                    project1(*at(i, k + 1))
                    turn1(*at(i, k - 1))
            turn1(0, LAST)
            turn1(1, LAST)

            pe.wait_ge(s_maxwide, 1)
            for b in range(2):
                ins = pe.matmul(bank[2][0:NP, b * C:(b + 1) * C], max_ab_wide[:, b, :], ident[0:C, 0:C],
                                start=True, stop=True)
            ins.then_inc(s_maxps, 1)
            pe.wait_ge(s_feats, 1)
            for i in range(NT):
                if i >= 2:
                    pe.wait_ge(s_fTsb, i - 1)
                pe.matmul(bank[i % 2][0:C, 0:NP], acc[:, i, :], ident[0:NP, 0:NP], is_transpose=True,
                          start=True, stop=True).then_inc(s_fT, 1)
                pe.wait_ge(s_fTsb, i + 1)
                if i >= 2:
                    pe.wait_ge(s_ysum, i - 1)
                pe.matmul(wide[i % 2][0:NP, 0:C], featsT[i % 2][:, :], wm[:, :], start=True, stop=True).then_inc(s_y, 1)

        @block.vector
        def _(dve):
            steps = [0]

            def then(ins):
                steps[0] += 1
                ins.then_inc(s_vec, 1)
                dve.wait_ge(s_vec, steps[0])

            def nodes_of(ap):
                return ap.unsqueeze(2).to_broadcast([NP, NT, C])

            def channels_of(ap):
                return ap.unsqueeze(1).to_broadcast([NP, NT, C])

            def edge_row(edge):
                then(dve.tensor_scalar(in_row[:, :], edge[:, :], float(HALF), float(1 - 2 * HALF), ALU.is_ge, ALU.mult))
                then(dve.scalar_tensor_tensor(tmp_n[:, :], edge[:, :], 2.0, in_row[:, :], ALU.mult, ALU.add))

            dve.memset(w5[:, :], 0.0).then_inc(s_wzero, 1)
            dve.memset(we[:, :], 0.0).then_inc(s_wzero, 1)
            dve.memset(zeros[:, :], 0.0).then_inc(s_zeros, 1)
            dve.memset(xT[C:C + 1, :], 1.0).then_inc(s_init, 1)
            dve.memset(start[:, :], 0.0).then_inc(s_start0, 1)
            for s in range(2):
                dve.memset(featsT[s][C:C + 1, :], 1.0)
            dve.memset(ones[:, :], 1.0)
            dve.memset(feat[0][:, :], 1.0)
            then(dve.memset(feat[1][:, :], 1.0))
            dve.wait_ge(s_nodes, 16 * 8)
            for k in range(2):
                dve.tensor_scalar(is_type[:, k, :], ntype_i[:, :], float(k), None, ALU.is_equal).then_inc(s_istype, 1)
            dve.wait_ge(s_iota, 2)
            dve.tensor_copy(lane[:, :], lane_i[:, :])
            then(dve.tensor_copy(node[:, :], node_i[:, :]))
            dve.wait_ge(s_keys, 32)
            for i in range(NT):
                ins = dve.tensor_scalar(le_row, keys[:, :], node[:, i:i + 1], 0.0, ALU.is_le, ALU.add,
                                        accum_out=full_rows[:, i:i + 1])
                then(ins)
            dve.tensor_copy(row_i[:, :], full_rows[:, :]).then_inc(s_row_i, 1)
            dve.wait_ge(s_istype, 2)
            for i in range(NT):
                dve.wait_ge(s_proj0, i + 1)
                dve.scalar_tensor_tensor(H[:, i, :], bank[i % 2][0:NP, 4 * C:8 * C], is_type[:, 1, i:i + 1], H[:, i, :],
                                         ALU.mult, ALU.add).then_inc(s_sel, 1)
            dve.wait_ge(s_edges, 48)
            dve.tensor_tensor(keep_r[:, :], dst_i[:, :], prev_i[:, :], ALU.is_equal).then_inc(s_rowlists, 1)
            then(dve.tensor_tensor(dst_step[:, :], prev_i[:, :], dst_i[:, :], ALU.subtract))
            dve.tensor_scalar(pen_r[:, :], dst_step[:, :], BIG, None, ALU.mult).then_inc(s_rowlists, 1)
            dve.tensor_copy(type_r[:, :], type_i[:, :]).then_inc(s_rowlists, 1)
            then(dve.tensor_copy(mid[:, :], mid_i[:, :]))
            then(dve.tensor_tensor(mid_same[:, :], mid[:, 0:1], mid[:, 1:2], ALU.is_equal))
            then(dve.tensor_scalar(cross[:, :], node[:, :], mid[:, 1:2], mid_same[:, :], ALU.is_equal, ALU.mult))
            then(dve.tensor_scalar(not_cross[:, :], cross[:, :], -1.0, 1.0, ALU.mult, ALU.add))
            dve.wait_ge(s_found, 16 * NT)
            then(dve.tensor_tensor(le[:, :, :], found[:, :, :], node[:, :].unsqueeze(2).to_broadcast([NP, NT, P]), ALU.is_le))
            then(dve.tensor_reduce(in_row[:, :], le[:, :, :], AX.X, ALU.add))
            dve.scalar_tensor_tensor(end[:, :], full_rows[:, :], float(P), in_row[:, :], ALU.mult, ALU.add).then_inc(s_end, 1)
            dve.wait_ge(s_end, 1)
            then(dve.tensor_copy(start[:, 1:NT], end[:, 0:NT - 1]))
            then(dve.tensor_scalar(last[:, :], end[:, :], -1.0, 0.0, ALU.add, ALU.max))
            edge_row(last)
            dve.tensor_copy(last_i[:, :], tmp_n[:, :]).then_inc(s_last_i, 1)
            dve.wait_ge(s_last_i, 1)
            then(dve.scalar_tensor_tensor(tmp_n[:, :], last[:, :], float(-HALF), cross[:, :], ALU.add, ALU.mult))
            dve.tensor_reduce(mb_col[:, :], tmp_n[:, :], AX.X, ALU.add).then_inc(s_mbcol, 1)
            dve.wait_ge(s_mbcol, 1)
            dve.wait_ge(s_shift, 16)
            then(dve.tensor_tensor(has_edges[:, :], end[:, :], start[:, :], ALU.is_gt))
            edge_row(start)
            then(dve.tensor_tensor(tmp_n[:, :], tmp_n[:, :], has_edges[:, :], ALU.mult))
            then(dve.tensor_scalar(in_row[:, :], has_edges[:, :], -1.0, 1.0, ALU.mult, ALU.add))
            then(dve.scalar_tensor_tensor(in_row[:, :], node[:, :], float(DUMP), in_row[:, :], ALU.add, ALU.mult))
            then(dve.tensor_tensor(tmp_n[:, :], tmp_n[:, :], in_row[:, :], ALU.add))
            dve.tensor_copy(first_i[:, :], tmp_n[:, :]).then_inc(s_first_i, 1)
            dve.wait_ge(s_mbps, 1)
            dve.tensor_tensor(mb_i[:, :], bank[2][0:C, 0:1], lane[:, :], ALU.add).then_inc(s_mb_i, 1)

            for s in range(2):
                dve.memset(h3d[s][:, :], 0.0)
                then(dve.memset(run[s][:, :], 0.0))
            dve.memset(feat[0][0:1, 0:1], 1.0).then_inc(s_ones, 1)
            dve.wait_ge(s_const, 16 * 4)

            def mask(s, r):
                dve.wait_ge(feat_in[s], 16 * 2 * (1 + T_EDGE) * (r + 1))
                dve.wait_ge(q2_ready[s], r)
                dve.scalar_tensor_tensor(featm[s][:, :], types[s][:, :], type_of_row[:, :], feat[s][:, :],
                                         ALU.is_equal, ALU.mult).then_inc(masked[s], 1)

            def scores(s, r, s_prev, r_prev):
                dve.wait_ge(keep_in[s], 32 * (r + 1))
                dve.wait_ge(injT[s], r + 1)
                dve.wait_ge(h3_ready[s_prev], r_prev + 1)
                dve.tensor_tensor_scan(h3d[s][:, :], keep[s][:, :], p_inj[s][:, :], h3d[s_prev][:, CH - 1:CH],
                                       ALU.mult, ALU.add).then_inc(h3_ready[s], 1)
                dve.wait_ge(h3_ready[s], r + 1)
                dve.wait_ge(q4_ready[s], r + 1)
                dve.wait_ge(num_ready[s], r)
                dve.tensor_tensor(prod[s][:, :], h3d[s][:, :], q4[s], ALU.mult).then_inc(prod_ready[s], 1)

            def differences(s, r):
                dve.wait_ge(scor_ready[s], r + 1)
                dve.wait_ge(exps_ready[s], r)
                dve.tensor_tensor(dif[s][:, :], scor[s][:, :], scor[s][:, :], ALU.subtract).then_inc(dif_ready[s], 1)

            def messages0(s, r, s_prev, r_prev):
                dve.wait_ge(exps_ready[s], r + 1)
                dve.reciprocal(inv[s][:, :], exps[s][:, :]).then_inc(inv_ready[s], 1)
                dve.wait_ge(inv_ready[s], r + 1)
                dve.tensor_tensor(prob[s][:, :], exps[s][:, :], inv[s][:, :], ALU.mult).then_inc(prob_ready[s], 1)
                dve.wait_ge(prob_ready[s], r + 1)
                dve.wait_ge(q2_ready[s], r + 1)
                dve.tensor_tensor(msg[s][:, :], prob[s][:, :], q2[s], ALU.mult).then_inc(msg_ready[s], 1)
                dve.wait_ge(msg_ready[s], r + 1)
                dve.wait_ge(run_ready[s_prev], r_prev + 1)
                dve.wait_ge(runT[s], r)
                dve.tensor_tensor_scan(run[s][:, :], keep[s][:, :], msg[s][:, :], run[s_prev][:, CH - 1:CH],
                                       ALU.mult, ALU.add).then_inc(run_ready[s], 1)

            LAST = CHUNKS // 2 - 1
            mask(0, 0)
            mask(1, 0)
            scores(0, 0, 1, -1)
            with dve.Fori(0, CHUNKS // 2 - 1) as i:
                for k in (1, 2):
                    differences(*at(i, k - 1))
                    if k == 1:
                        mask(*at(i, k + 1))
                    scores(*at(i, k), *at(i, k - 1))
                    messages0(*at(i, k - 1), (k - 2) % 2, i + (k - 2) // 2)
                    if k == 2:
                        mask(*at(i, k + 1))
            differences(0, LAST)
            scores(1, LAST, 0, LAST)
            messages0(0, LAST, 1, LAST - 1)
            differences(1, LAST)
            messages0(1, LAST, 0, LAST)

            def layer_norm(src, round_):
                then(dve.tensor_reduce(mean[:, :], src[:, :, :], AX.X, ALU.add))
                then(dve.tensor_scalar(mean[:, :], mean[:, :], 1.0 / C, None, ALU.mult))
                then(dve.tensor_tensor(src[:, :, :], src[:, :, :], nodes_of(mean[:, :]), ALU.subtract))
                then(dve.tensor_tensor(sq[:, :, :], src[:, :, :], src[:, :, :], ALU.mult))
                then(dve.tensor_reduce(var[:, :], sq[:, :, :], AX.X, ALU.add))
                dve.tensor_scalar(var[:, :], var[:, :], 1.0 / C, LN_EPS, ALU.mult, ALU.add).then_inc(s_acc0, 1)
                dve.wait_ge(s_sqrt, round_)
                then(dve.reciprocal(rstd[:, :], std[:, :]))
                return dve.tensor_tensor(x1[:, :, :], src[:, :, :], nodes_of(rstd[:, :]), ALU.mult)

            then(dve.tensor_tensor(acc[:, :, :], x_sb[:, :, :], H[:, :, 0:C], ALU.add))
            dve.wait_ge(s_cut0, 16)
            then(dve.tensor_tensor(sq[:, :, :], channels_of(cut0[:, :]), nodes_of(cross[:, :]), ALU.mult))
            dve.wait_ge(s_got0, 16 * NT)
            then(dve.tensor_tensor(got0[:, :, :], got0[:, :, :], nodes_of(has_edges[:, :]), ALU.mult))
            then(dve.tensor_tensor(got0[:, :, :], got0[:, :, :], sq[:, :, :], ALU.add))
            then(dve.tensor_tensor(acc[:, :, :], acc[:, :, :], got0[:, :, :], ALU.add))
            layer_norm(acc, 1).then_inc(s_x1, 1)
            dve.wait_ge(s_x1, 1)

            for s in range(2):
                dve.memset(feat[s][:, :], 1.0)
                dve.memset(run_s[s][:, :], 0.0)
                dve.memset(run_n[s][:, :], 0.0)
                then(dve.memset(runmax[s][:, :], 0.0))
            dve.memset(mean[:, :], 0.0).then_inc(s_ones1, 1)

            def maxima(s, r, s_prev, r_prev):
                dve.wait_ge(max_out[s], 16 * r)
                dve.wait_ge(max_ready[s_prev], r_prev + 1)
                dve.tensor_copy(runmax[s][:, 0:1], runmax[s_prev][:, CH:CH + 1]).then_inc(carry_ready[s], 1)
                dve.wait_ge(pen_in[s], 32 * (r + 1))
                dve.wait_ge(m_ready[s], r + 1)
                dve.tensor_tensor_scan(runmax[s][:, 1:CH + 1], keep[s][:, :], m[s][:, :], runmax[s_prev][:, CH:CH + 1],
                                       ALU.add, ALU.max).then_inc(max_ready[s], 1)
                dve.wait_ge(carry_ready[s], r + 1)
                dve.wait_ge(max_ready[s], r + 1)
                dve.wait_ge(updown_ready[s], 2 * r)
                dve.tensor_tensor(y[s][:, :], runmax[s][:, 0:CH], keep[s][:, :], ALU.add).then_inc(shift_ready[s], 1)
                dve.wait_ge(shift_ready[s], r + 1)
                dve.tensor_tensor(y[s][:, :], m[s][:, :], y[s][:, :], ALU.subtract).then_inc(y_ready[s], 1)

            def sums(s, r, s_prev, r_prev):
                dve.wait_ge(expm_ready[s], r + 1)
                dve.tensor_tensor(mexp[s][:, :], m[s][:, :], expm[s][:, :], ALU.mult).then_inc(mexp_ready[s], 1)
                dve.wait_ge(decay_ready[s], r + 1)
                dve.wait_ge(run1T[s], r)
                dve.wait_ge(s_run[s_prev], r_prev + 1)
                dve.tensor_tensor_scan(run_s[s][:, :], decay[s][:, :], expm[s][:, :], run_s[s_prev][:, CH - 1:CH],
                                       ALU.mult, ALU.add).then_inc(s_run[s], 1)
                dve.wait_ge(mexp_ready[s], r + 1)
                dve.wait_ge(n_run[s_prev], r_prev + 1)
                dve.tensor_tensor_scan(run_n[s][:, :], decay[s][:, :], mexp[s][:, :], run_n[s_prev][:, CH - 1:CH],
                                       ALU.mult, ALU.add).then_inc(n_run[s], 1)

            maxima(0, 0, 1, -1)
            with dve.Fori(0, CHUNKS // 2 - 1) as i:
                for k in (1, 2):
                    maxima(*at(i, k), *at(i, k - 1))
                    sums(*at(i, k - 1), (k - 2) % 2, i + (k - 2) // 2)
            maxima(1, LAST, 0, LAST)
            sums(0, LAST, 1, LAST - 1)
            sums(1, LAST, 0, LAST)

            dve.wait_ge(s_mb, 16)
            then(dve.tensor_copy(max_ab[:, 0:1], runmax[1][0:C, CH:CH + 1]))
            dve.tensor_copy(max_ab_wide[:, :, :], max_ab[:, :].unsqueeze(2).to_broadcast([C, 2, NP])).then_inc(s_maxwide, 1)
            dve.wait_ge(s_maxps, 1)
            then(dve.tensor_copy(mx[:, :, :], bank[2][0:NP, 0:2 * C].rearrange("p (q c) -> p q c", q=2)))
            then(dve.tensor_tensor(mm[:, :], mx[:, 0, :], mx[:, 1, :], ALU.max))
            dve.tensor_tensor(dmx[:, :, :], mx[:, :, :], mm[:, :].unsqueeze(1).to_broadcast([NP, 2, C]), ALU.subtract).then_inc(s_dmx, 1)
            dve.wait_ge(s_wgt, 1)
            dve.wait_ge(s_cut1, 16)
            then(dve.tensor_tensor(scale_b[:, :, :], channels_of(wgt[:, 1, :]), nodes_of(cross[:, :]), ALU.mult))
            then(dve.tensor_tensor(scale_b[:, :, :], scale_b[:, :, :], nodes_of(not_cross[:, :]), ALU.add))
            then(dve.tensor_tensor(cut1[:, :, :], cut1[:, :, :], wgt[:, 0:1, :].to_broadcast([NP, 2, C]), ALU.mult))
            dve.wait_ge(s_got1, 16 * NT)
            for q, part in ((0, sq), (1, got0)):
                then(dve.tensor_tensor(part[:, :, :], channels_of(cut1[:, q, :]), nodes_of(cross[:, :]), ALU.mult))
                then(dve.tensor_tensor(got1[:, :, q, :], got1[:, :, q, :], scale_b[:, :, :], ALU.mult))
                then(dve.tensor_tensor(part[:, :, :], got1[:, :, q, :], part[:, :, :], ALU.add))
            then(dve.reciprocal(sq[:, :, :], sq[:, :, :]))
            then(dve.tensor_tensor(got0[:, :, :], got0[:, :, :], sq[:, :, :], ALU.mult))
            then(dve.tensor_tensor(got0[:, :, :], got0[:, :, :], nodes_of(has_edges[:, :]), ALU.mult))
            dve.tensor_tensor(acc[:, :, :], x1[:, :, :], got0[:, :, :], ALU.add).then_inc(s_feats, 1)
            for i in range(NT):
                dve.wait_ge(s_y, i + 1)
                dve.tensor_tensor(y_out[:, i, :], wide[i % 2][0:NP, 0:C], x1[:, i, :], ALU.add).then_inc(s_ysum, 1)
            dve.wait_ge(s_ysum, NT)
            layer_norm(y_out, 2).then_inc(s_fin, 1)
            dve.wait_ge(s_fin, 1)


def kernel(x, src, dst, edge_attr_16, edge_attr_32, edge_type_3, node_type_2,
           L0_gnn_W1, L0_gnn_b1, L0_gnn_W2, L0_gnn_b2, L0_gnn_W3, L0_gnn_b3, L0_gnn_W4, L0_gnn_b4,
           L0_gnn_W5, L0_gnn_b5, L1_gnn_We, L1_gnn_be, L1_gnn_Wm, L1_gnn_bm):
    import numpy as np
    import concourse.bacc as bacc
    from concourse.bass_utils import run_bass_kernel_spmd as run

    def padded(a, value):
        return np.concatenate([np.asarray(a), np.full(EP - N_EDGES, value, np.int32)])

    def features(a):
        a = np.asarray(a).T
        return np.concatenate([a, np.zeros((a.shape[0], EP - N_EDGES), a.dtype)], axis=1)

    dst_p = padded(dst, N_NODES)
    src_p = padded(src, 0)
    row = np.arange(P) % C
    type_of_row = np.where(row < T_EDGE * F0, row // F0, np.where(row < T_EDGE * (F0 + 1), row - T_EDGE * F0, -1))
    arrays = {
        "x": x, "xT": np.asarray(x).T,
        "src": src_p.reshape(2, CHUNKS, P, TILES).transpose(1, 2, 0, 3).reshape(CHUNKS * P, 2 * TILES),
        "dst": dst_p.reshape(ROWS, P),
        "dst_prev": np.concatenate([np.full(1, -1, np.int32), dst_p[:-1]]).reshape(P, ROWS),
        "keys": dst_p[P - 1::P].reshape(1, ROWS),
        "mid": dst_p[HALF - 1:HALF + 1].reshape(1, 2),
        "etype": padded(edge_type_3, 0).reshape(P, ROWS),
        "node_type": np.asarray(node_type_2).reshape(NP, NT),
        "ea16T": features(edge_attr_16), "ea32T": features(edge_attr_32),
        "W1": L0_gnn_W1, "b1": L0_gnn_b1, "W3": L0_gnn_W3, "b3": L0_gnn_b3,
        "W24": np.stack([L0_gnn_W2, L0_gnn_W4], axis=-1).reshape(2, C, 2 * C),
        "b24": np.stack([L0_gnn_b2, L0_gnn_b4], axis=-1).reshape(2, 2 * C),
        "W5": L0_gnn_W5, "b5": L0_gnn_b5,
        "We": L1_gnn_We, "be": np.asarray(L1_gnn_be).reshape(1, C),
        "Wm": L1_gnn_Wm, "bm": np.asarray(L1_gnn_bm).reshape(1, C),
        "ident": np.eye(P, dtype=np.float32),
        "half_ones": np.kron(np.eye(2), np.ones((C, C))).astype(np.float32),
        "type_of_row": type_of_row.astype(np.float32).reshape(P, 1),
    }
    nc = bacc.Bacc("TRN2", target_bir_lowering=False, num_devices=1)
    feed, aps = {}, {}
    for name, a in arrays.items():
        a = np.ascontiguousarray(a)
        feed[f"in_{name}"] = a
        aps[name] = nc.dram_tensor(f"in_{name}", a.shape, mybir.dt.from_np(a.dtype), kind="ExternalInput").ap()
    out = nc.dram_tensor("out", (N_NODES, C), mybir.dt.float32, kind="ExternalOutput").ap()
    gnn_program(nc, aps, out)
    return run(nc, [feed], core_ids=[0]).results[0]["out"]
```

```python
import concourse.bass as bass
from concourse import mybir
from contextlib import ExitStack

N_NODES = 3125
N_EDGES = 100000
C = 64
F0, F1 = 16, 32
T_EDGE = 3
P = 128
NP = 125
NT = N_NODES // NP
CH = 512
TILES = CH // P
CHUNKS = 2 * -(-N_EDGES // (4 * CH))
HALF = CHUNKS * CH
EP = 2 * HALF
ROWS = EP // P
CUT_ROW = 2 * (HALF - 1)
DUMP = EP
EPS = 1e-7
LN_EPS = 1e-5
GROUPS = 5
GT = NT // GROUPS
W_ORDER = ((C, 3 * C), (3 * C, 4 * C), (0, C))
BIG = 1e30


def gnn_program(nc, t, out):
    f32, bf16, i32 = mybir.dt.float32, mybir.dt.bfloat16, mybir.dt.int32
    ALU, ACT, AX = mybir.AluOpType, mybir.ActivationFunctionType, mybir.AxisListType
    ctx = ExitStack()
    with ctx:
        def sb(name, shape, dt=f32):
            return ctx.enter_context(nc.sbuf_tensor(name, shape, dt))

        def pb(name, cols):
            return ctx.enter_context(nc.psum_tensor(name, [P, cols], f32))

        def sem(name):
            return ctx.enter_context(nc.semaphore(name))

        def sems(name):
            return [sem(f"{name}_{s}") for s in range(2)]

        def scratch(name, shape, dt=f32):
            return nc.dram_tensor(name, shape, dt).ap()

        d_keep = scratch("d_keep", [1, EP], bf16)
        d_pen = scratch("d_pen", [1, EP], bf16)
        d_type = scratch("d_type", [1, EP], bf16)
        d_h24 = scratch("d_h24", [N_NODES, 2 * C])
        d_h3 = scratch("d_h3", [N_NODES, C])
        d_inj = scratch("d_inj", [EP + NP * NT, C])
        d_run0 = scratch("d_run0", [EP, C])
        d_x1 = scratch("d_x1", [N_NODES, C])
        d_run1 = scratch("d_run1", [EP, 2 * C])
        d_max = scratch("d_max", [C * HALF, 1])

        ident = sb("ident", [P, P])
        half_sum = sb("half_sum", [P, 2])
        type_of_row = sb("type_of_row", [P, 1])
        ones = sb("ones", [NP, C])
        zeros = sb("zeros", [P, 1792])
        w_nodes = sb("w_nodes", [C + 1, 2, 4 * C])
        w5 = sb("w5", [P, P])
        we = sb("we", [P, P])
        wm = sb("wm", [C + 1, C])
        xT = sb("xT", [C + 1, N_NODES])
        typed = [sb(f"typed{k}", [NP, 2, NT, C]) for k in range(2)]
        x_typed = [b[0:C + 1, :, :, :].rearrange("p a i c -> p (a i c)")[:, 0:N_NODES]
                   for b in typed]
        x_sb = sb("x_sb", [NP, NT, C])
        H = sb("H", [NP, NT, 4 * C])
        node_i = sb("node_i", [NP, NT], i32)
        node = sb("node", [NP, NT])
        keys = sb("keys", [NP, ROWS], i32)
        keys16 = sb("keys16", [NP, ROWS], mybir.dt.int16)
        full_rows = sb("full_rows", [NP, NT])
        row_i = sb("row_i", [NP, NT], i32)
        found = sb("found", [NP, NT, P], i32)
        ntype_i = found[0:C + 1, :, :].rearrange("p i k -> p (i k)")[:, 0:N_NODES]
        le = sb("le", [NP, NT, P], bf16)
        le_rows = [le[:, :, :].rearrange("p i k -> p (i k)")[:, k * ROWS:(k + 1) * ROWS] for k in range(4)]
        in_row = sb("in_row", [NP, NT])
        end = sb("end", [NP, NT])
        start = sb("start", [NP, NT])
        has_edges = sb("has_edges", [NP, NT])
        last = sb("last", [NP, NT])
        last_i = sb("last_i", [NP, NT], i32)
        tmp_n = sb("tmp_n", [NP, NT])
        first_i = sb("first_i", [NP, NT], i32)
        mid_i = sb("mid_i", [NP, 2], i32)
        mid = sb("mid", [NP, 2])
        mid_same = sb("mid_same", [NP, 1])
        cross = sb("cross", [NP, NT])
        not_cross = sb("not_cross", [NP, NT])
        fix = sb("fix", [16, C])
        mb_col = sb("mb_col", [NP, 1])
        lane_i = sb("lane_i", [C, 1], i32)
        lane = sb("lane", [C, 1])
        mb_i = sb("mb_i", [C, 1], i32)
        max_ab = sb("max_ab", [C, 2])
        max_ab_wide = sb("max_ab_wide", [C, 2, NP])
        dst_i = sb("dst_i", [P, ROWS], i32)
        prev_i = sb("prev_i", [P, ROWS], i32)
        type_i = sb("type_i", [P, ROWS], i32)
        dst_step = sb("dst_step", [P, ROWS])
        keep_r = sb("keep_r", [P, ROWS], bf16)
        pen_r = sb("pen_r", [P, ROWS], bf16)
        type_r = sb("type_r", [P, ROWS], bf16)
        idx = [sb(f"idx{s}", [P, 2 * TILES], i32) for s in range(2)]
        rows0 = [sb(f"rows0_{s}", [P, TILES, 2, 2 * C]) for s in range(2)]
        rows1 = [r[:, :, :, :].rearrange("p j h c -> p (j h c)")[:, 0:TILES * 2 * C].rearrange("p (j h c) -> p j h c", j=TILES, h=2)
                 for r in rows0]
        types = [sb(f"types{s}", [P, CH], bf16) for s in range(2)]
        feat = [sb(f"feat{s}", [P, CH]) for s in range(2)]
        featm = [sb(f"featm{s}", [P, CH]) for s in range(2)]
        keep = [sb(f"keep{s}", [P, CH], bf16) for s in range(2)]
        inj = [sb(f"inj{s}", [P, TILES, 2 * C]) for s in range(2)]
        keep_late = [sb(f"keep_late{s}", [P, CH], bf16) for s in range(2)]
        h3d = [sb(f"h3d{s}", [P, CH]) for s in range(2)]
        prod = [sb(f"prod{s}", [P, CH]) for s in range(2)]
        q2_sb = [sb(f"q2_sb{s}", [P, CH]) for s in range(2)]
        prob_wide = [sb(f"prob_wide{s}", [P, TILES, 2, C]) for s in range(2)]
        msg = [sb(f"msg{s}", [P, CH]) for s in range(2)]
        run = [sb(f"run{s}", [P, CH]) for s in range(2)]
        score, diff, expo, prob = ([sb(f"{n}{s}", [P, TILES, 2, 1]) for s in range(2)] for n in ("score", "diff", "expo", "prob"))
        top, total, inv = ([sb(f"{n}{s}", [P, TILES, 2]) for s in range(2)] for n in ("top", "total", "inv"))
        stage0 = [sb(f"stage0_{s}", [P, TILES, 2 * C]) for s in range(2)]
        relu, m, y, down, mexp = prod, h3d, q2_sb, msg, run
        up = [w[:, :, :, :].rearrange("p j h c -> p (j h c)") for w in prob_wide]
        decay = featm
        expm = [sb(f"expm{s}", [P, CH]) for s in range(2)]
        runmax = [sb(f"runmax{s}", [P, CH + 1]) for s in range(2)]
        run_s = [sb(f"run_s{s}", [P, CH]) for s in range(2)]
        run_n = [sb(f"run_n{s}", [P, CH]) for s in range(2)]
        stage1 = [sb(f"stage1_{s}", [P, TILES, 2, 2, C]) for s in range(2)]
        (acc, x1), (sq, got0) = ([b[:, a, :, :] for a in range(2)] for b in typed)
        cut0 = sb("cut0", [NP, C])
        mean = sb("mean", [NP, NT])
        var = sb("var", [NP, NT])
        std = sb("std", [NP, NT])
        rstd = sb("rstd", [NP, NT])
        got1 = H[:, :, 0:2 * C].rearrange("p i (q c) -> p i q c", q=2)
        cut1 = sb("cut1", [NP, 2, C])
        mx = sb("mx", [NP, 2, C])
        mm = sb("mm", [NP, C])
        dmx = sb("dmx", [NP, 2, C])
        wgt = sb("wgt", [NP, 2, C])
        scale_b = found[:, :, 0:C].bitcast(f32)
        featsT = [sb(f"featsT{s}", [C + 1, NP]) for s in range(2)]
        y_out = found[:, :, C:2 * C].bitcast(f32)

        wide = [pb(f"wide{s}", 2 * CH) for s in range(2)]
        bank = [pb(f"bank{b}", CH) for b in range(4)]
        q2 = [w[:, 0:CH] for w in wide]
        q4 = [w[:, CH:2 * CH] for w in wide]
        p_inj, p_num, p_prob, p_out0 = bank
        p_m, p_out1 = bank[0:2], wide

        s_const, s_nodes, s_edges = sem("s_const"), sem("s_nodes"), sem("s_edges")
        s_wzero, s_weights, s_ones = sem("s_wzero"), sem("s_weights"), sem("s_ones")
        s_keys, s_iota, s_zeros = sem("s_keys"), sem("s_iota"), sem("s_zeros")
        s_typed, s_proj, s_sel = sem("s_typed"), sem("s_proj"), sem("s_sel")
        s_h24, s_h3, s_rowlists, s_lists = sem("s_h24"), sem("s_h3"), sem("s_rowlists"), sem("s_lists")
        s_row_i, s_found, s_end, s_shift = sem("s_row_i"), sem("s_found"), sem("s_end"), sem("s_shift")
        s_first_i, s_last_i, s_injzero, s_inj = sem("s_first_i"), sem("s_last_i"), sem("s_injzero"), sem("s_inj")
        s_fix, s_fixed, s_mbcol, s_mbps, s_mb_i = sem("s_fix"), sem("s_fixed"), sem("s_mbcol"), sem("s_mbps"), sem("s_mb_i")
        s_vec = sem("s_vec")
        s_chunks = sem("s_chunks")
        idx_in, got_rows, feat_in, keep_in, inj_in = sems("idx_in"), sems("got_rows"), sems("feat_in"), sems("keep_in"), sems("inj_in")
        masked, q4_ready, q2_ready, injT = sems("masked"), sems("q4_ready"), sems("q2_ready"), sems("injT")
        keep_copied, q2_copied, h3_ready, prod_ready = sems("keep_copied"), sems("q2_copied"), sems("h3_ready"), sems("prod_ready")
        num_ready, score_ready, diff_ready = sems("num_ready"), sems("score_ready"), sems("diff_ready")
        exps_ready, prob_ready = sems("exps_ready"), sems("prob_ready")
        softmax_step = sems("softmax_step")
        wide_ready, probT, msg_ready = sems("wide_ready"), sems("probT"), sems("msg_ready")
        run_ready, runT, staged, stored = sems("run_ready"), sems("runT"), sems("staged"), sems("stored")
        s_cut0, s_square, s_squared, s_var, s_sqrt, s_x1, s_x1_out = (sem("s_cut0"), sem("s_square"), sem("s_squared"),
                                                                      sem("s_var"), sem("s_sqrt"), sem("s_x1"), sem("s_x1_out"))
        s_got0 = [sem(f"s_got0_{g}") for g in range(GROUPS)]
        s_got1 = [sem(f"s_got1_{g}") for g in range(GROUPS)]
        idx1_in, got1_rows, feat1_in, pen_in = sems("idx1_in"), sems("got1_rows"), sems("feat1_in"), sems("pen_in")
        z_ready, relu_ready, m_ready = sems("z_ready"), sems("relu_ready"), sems("m_ready")
        max_ready = sems("max_ready")
        shift_ready, y_ready = sems("shift_ready"), sems("y_ready")
        updown_ready, decay_ready, expm_ready = sems("updown_ready"), sems("decay_ready"), sems("expm_ready")
        mexp_ready, s_run, n_run, run1T, staged1, stored1, max_out = (sems("mexp_ready"), sems("s_run"), sems("n_run"),
                                                                     sems("run1T"), sems("staged1"), sems("stored1"), sems("max_out"))
        s_ones1 = sem("s_ones1")
        s_cut1, s_mb, s_maxwide, s_maxps, s_dmx, s_wgt = (sem("s_cut1"), sem("s_mb"), sem("s_maxwide"),
                                                                  sem("s_maxps"), sem("s_dmx"), sem("s_wgt"))
        s_feats, s_fT, s_fTsb, s_y, s_ysum, s_fin, s_out = (sem("s_feats"), sem("s_fT"), sem("s_fTsb"), sem("s_y"),
                                                           sem("s_ysum"), sem("s_fin"), sem("s_out"))

        block = ctx.enter_context(nc.Block())

        PEELED = 4

        def peeled(c):
            return (c % 2, c // 2, c) if 0 <= c < CHUNKS else None

        def steps(eng, step, before, after, first=PEELED):
            for c in range(-before, first):
                step(lambda d: peeled(c + d))
            stop = CHUNKS - after - (CHUNKS - after) % 2
            with eng.Fori(first // 2, stop // 2) as i:
                for k in range(2):
                    step(lambda d: ((k + d) % 2, i + (k + d) // 2, 2 * i + k + d))
            for c in range(stop, CHUNKS + after):
                step(lambda d: peeled(c + d))

        def wait(eng, semaphore, count):
            if not (isinstance(count, int) and count == 0):
                eng.wait_ge(semaphore, count)

        @block.sync
        def _(sp):
            sp.dma_start(ntype_i, t["node_type"].to_broadcast([C + 1, N_NODES])).then_inc(s_nodes, 16)
            sp.dma_start(xT[0:C, :], t["xT"]).then_inc(s_nodes, 16)
            sp.dma_start(keys[:, :], t["keys"].to_broadcast([NP, ROWS])).then_inc(s_keys, 16)
            sp.dma_start(mid_i[:, :], t["mid"].to_broadcast([NP, 2])).then_inc(s_keys, 16)
            for name, a, b in (("24", C, 3 * C), ("3", 3 * C, 4 * C), ("1", 0, C)):
                sp.dma_start(w_nodes[0:C, :, a:b], t["W" + name].rearrange("t f h -> f t h")).then_inc(s_nodes, 16)
                sp.dma_start(w_nodes[C:C + 1, :, a:b], t["b" + name].rearrange("(a t) h -> a t h", a=1)).then_inc(s_nodes, 16)
            sp.dma_start(dst_i[:, :], t["dst"].rearrange("a b -> (a b)").rearrange("(p k) -> p k", p=P)).then_inc(s_edges, 16)
            sp.dma_start(prev_i[:, :], t["dst_prev"]).then_inc(s_edges, 16)
            sp.dma_start(type_i[:, :], t["etype"]).then_inc(s_edges, 16)
            sp.dma_start(ident[:, :], t["ident"]).then_inc(s_const, 16)
            sp.dma_start(half_sum[:, :], t["half_sum"]).then_inc(s_const, 16)
            sp.dma_start(type_of_row[:, :], t["type_of_row"]).then_inc(s_const, 16)
            sp.dma_start(x_sb[:, :, :], t["x"].rearrange("(p i) c -> p i c", i=NT)).then_inc(s_const, 16)
            sp.wait_ge(s_wzero, 2)
            for h in range(2):
                b = h * C
                sp.dma_start(w5[b:b + T_EDGE * F0, b:b + C], t["W5"].rearrange("t f h -> (t f) h")).then_inc(s_weights, 16)
                sp.dma_start(w5[b + T_EDGE * F0:b + T_EDGE * (F0 + 1), b:b + C], t["b5"]).then_inc(s_weights, 16)
                sp.dma_start(we[b:b + F1, b:b + C], t["We"]).then_inc(s_weights, 16)
                sp.dma_start(we[b + F1:b + F1 + 1, b:b + C], t["be"]).then_inc(s_weights, 16)
            sp.dma_start(wm[0:C, :], t["Wm"]).then_inc(s_weights, 16)
            sp.dma_start(wm[C:C + 1, :], t["bm"]).then_inc(s_weights, 16)

            def offsets(c):
                return sp.snap(c * P), sp.snap(c * (2 * CH)), [sp.snap(c * CH), sp.snap(c * CH + HALF)]

            def load_src(s, r, of_src, used_up, landed):
                wait(sp, used_up[s], 16 * 2 * TILES * r)
                sp.dma_start(idx[s][:, :], t["src"][bass.ds(of_src, P), :]).then_inc(landed[s], 16)

            def load_features0(s, r, of_edge):
                wait(sp, masked[s], r)
                for h in range(2):
                    sp.dma_start(types[s][h * C:(h + 1) * C, :],
                                 d_type[:, bass.ds(of_edge[h], CH)].to_broadcast([C, CH])).then_inc(feat_in[s], 16)
                    sp.dma_start(feat[s][h * C:h * C + T_EDGE * F0, :],
                                 t["ea16x3T"][:, bass.ds(of_edge[h], CH)]).then_inc(feat_in[s], 16)

            def load_keep(s, r, of_edge):
                wait(sp, keep_copied[s], r)
                wait(sp, h3_ready[s], r)
                for h in range(2):
                    sp.dma_start(keep[s][h * C:(h + 1) * C, :],
                                 d_keep[:, bass.ds(of_edge[h], CH)].to_broadcast([C, CH])).then_inc(keep_in[s], 16)

            def load_inj(s, r, of_inj):
                wait(sp, injT[s], r)
                sp.dma_start(inj[s][:, :, :], d_inj[bass.ds(of_inj, 2 * CH), :]
                             .rearrange("(p j h) c -> p j (h c)", j=TILES, h=2)).then_inc(inj_in[s], 16)

            for s in range(2):
                load_src(s, 0, s * P, got_rows, idx_in)
            sp.wait_ge(s_sel, NT)
            sp.dma_start(d_h24.rearrange("(p i) c -> p i c", i=NT), H[:, :, C:3 * C]).then_inc(s_h24, 16)
            sp.wait_ge(s_rowlists, 3)
            for dst, src in ((d_keep, keep_r), (d_pen, pen_r), (d_type, type_r)):
                sp.dma_start(dst.rearrange("a (p b) -> (a p) b", p=P), src[:, :]).then_inc(s_lists, 16)
            sp.wait_ge(s_sel, 2 * NT)
            sp.dma_start(d_h3.rearrange("(p i) c -> p i c", i=NT), H[:, :, 3 * C:4 * C]).then_inc(s_h3, 16)
            sp.wait_ge(s_lists, 48)
            sp.wait_ge(s_ones, 1)
            for s in range(2):
                load_features0(s, 0, [s * CH, s * CH + HALF])
                load_keep(s, 0, [s * CH, s * CH + HALF])
            sp.wait_ge(s_end, 1)
            sp.dma_start(start[1:NP, 0:1], end[0:NP - 1, NT - 1:NT]).then_inc(s_shift, 16)
            sp.wait_ge(s_fix, 16)
            sp.wait_ge(s_inj, 16 * NT)
            sp.dma_start(d_inj[1:2, :], fix[0:1, :]).then_inc(s_fixed, 16)
            sp.wait_ge(s_fixed, 16)
            for s in range(2):
                load_inj(s, 0, s * (2 * CH))

            with sp.Fori(1, CHUNKS // 2) as i:
                for s in range(2):
                    of_src, of_inj, of_edge = offsets(2 * i + s)
                    load_src(s, i, of_src, got_rows, idx_in)
                    load_features0(s, i, of_edge)
                    load_inj(s, i, of_inj)
                    load_keep(s, i, of_edge)

            for s in range(2):
                sp.wait_ge(stored[s], 16 * (CHUNKS // 2))
            sp.dma_start(cut0[:, :], d_run0[CUT_ROW:CUT_ROW + 1, :].to_broadcast([NP, C])).then_inc(s_cut0, 16)

            def load_features1(s, r, of_edge):
                wait(sp, z_ready[s], r)
                for h in range(2):
                    sp.dma_start(feat[s][h * C:h * C + F1, :],
                                 t["ea32T"][:, bass.ds(of_edge[h], CH)]).then_inc(feat1_in[s], 16)

            def load_pen(s, r, of_edge):
                sp.wait_ge(s_lists, 48)
                wait(sp, shift_ready[s], r)
                for h in range(2):
                    sp.dma_start(keep[s][h * C:(h + 1) * C, :],
                                 d_pen[:, bass.ds(of_edge[h], CH)].to_broadcast([C, CH])).then_inc(pen_in[s], 16)

            sp.wait_ge(s_ones1, 1)
            for s in range(2):
                sp.wait_ge(got_rows[s], 16 * 2 * TILES * (CHUNKS // 2))
                sp.dma_start(idx[s][:, :], t["src"][s * P:(s + 1) * P, :]).then_inc(idx1_in[s], 16)
                load_features1(s, 0, [s * CH, s * CH + HALF])
                load_pen(s, 0, [s * CH, s * CH + HALF])
            for g in range(GROUPS):
                sp.wait_ge(s_x1, g + 1)
                sp.dma_start(d_x1.rearrange("(p i) c -> p i c", i=NT)[:, g * GT:(g + 1) * GT, :],
                             x1[:, g * GT:(g + 1) * GT, :]).then_inc(s_x1_out, 16)
            with sp.Fori(1, CHUNKS // 2) as i:
                for s in range(2):
                    of_src, _, of_edge = offsets(2 * i + s)
                    load_src(s, i, of_src, got1_rows, idx1_in)
                    load_features1(s, i, of_edge)
                    load_pen(s, i, of_edge)

            for s in range(2):
                sp.wait_ge(stored1[s], 16 * (CHUNKS // 2))
            sp.dma_start(cut1[:, :, :], d_run1[CUT_ROW:CUT_ROW + 1, :].rearrange("a (q c) -> a q c", q=2).to_broadcast([NP, 2, C])).then_inc(s_cut1, 16)
            for g in range(GROUPS):
                sp.wait_ge(s_fin, g + 1)
                sp.dma_start(out.rearrange("(p i) c -> p i c", i=NT)[:, g * GT:(g + 1) * GT, :],
                             x1[:, g * GT:(g + 1) * GT, :]).then_inc(s_out, 16)
            sp.wait_ge(s_out, 16 * GROUPS)

        @block.gpsimd
        def _(pool):
            pool.iota(node_i[:, :], pattern=[[1, NT]], base=0, channel_multiplier=NT).then_inc(s_iota, 1)
            pool.iota(lane_i[:, :], pattern=[[0, 1]], base=0, channel_multiplier=HALF).then_inc(s_iota, 1)
            pool.wait_ge(s_row_i, 1)
            for i in range(NT):
                pool.indirect_dma_start(out=found[:, i, :], out_offset=None, in_=t["dst"],
                                        in_offset=bass.IndirectOffsetOnAxis(ap=row_i[:, i:i + 1], axis=0)).then_inc(s_found, 16)

            def gather(s, r, begun, landed_idx, used_up, dst, table, landed):
                pool.wait_ge(landed_idx[s], 16 * (r + 1))
                wait(pool, used_up[s], r)
                pool.sem_inc(begun, 1)
                for j in range(2 * TILES):
                    pool.indirect_dma_start(out=dst[s][:, j % TILES, j // TILES, :], out_offset=None, in_=table,
                                            in_offset=bass.IndirectOffsetOnAxis(ap=idx[s][:, j:j + 1], axis=0)).then_inc(landed[s], 16)

            pool.wait_ge(s_h24, 16)
            for s in range(2):
                gather(s, 0, s_chunks, idx_in, q2_ready, rows0, d_h24, got_rows)
            pool.wait_ge(s_h3, 16)
            pool.indirect_dma_start(out=fix[:, :], out_offset=None, in_=d_h3,
                                    in_offset=bass.IndirectOffsetOnAxis(ap=mid_i[0:16, 1:2], axis=0)).then_inc(s_fix, 16)
            pool.wait_ge(s_injzero, 16 * 28)
            pool.wait_ge(s_first_i, 1)
            for i in range(NT):
                pool.indirect_dma_start(out=d_inj, out_offset=bass.IndirectOffsetOnAxis(ap=first_i[:, i:i + 1], axis=0),
                                        in_=H[:, i, 3 * C:4 * C], in_offset=None).then_inc(s_inj, 16)
            with pool.Fori(1, CHUNKS // 2) as i:
                for s in range(2):
                    gather(s, i, s_chunks, idx_in, q2_ready, rows0, d_h24, got_rows)
            pool.wait_ge(s_last_i, 1)
            for s in range(2):
                pool.wait_ge(stored[s], 16 * (CHUNKS // 2))
            for i in range(NT):
                pool.indirect_dma_start(out=got0[:, i, :], out_offset=None, in_=d_run0,
                                        in_offset=bass.IndirectOffsetOnAxis(ap=last_i[:, i:i + 1], axis=0)).then_inc(s_got0[i // GT], 16)
            pool.wait_ge(s_x1_out, 16 * GROUPS)
            for s in range(2):
                gather(s, 0, s_chunks, idx1_in, z_ready, rows1, d_x1, got1_rows)
            with pool.Fori(1, CHUNKS // 2) as i:
                for s in range(2):
                    gather(s, i, s_chunks, idx1_in, z_ready, rows1, d_x1, got1_rows)
            pool.wait_ge(s_mb_i, 1)
            for s in range(2):
                pool.wait_ge(max_out[s], 16 * (CHUNKS // 2))
            pool.indirect_dma_start(out=max_ab[:, 1:2], out_offset=None, in_=d_max,
                                    in_offset=bass.IndirectOffsetOnAxis(ap=mb_i[:, 0:1], axis=0)).then_inc(s_mb, 16)
            for s in range(2):
                pool.wait_ge(stored1[s], 16 * (CHUNKS // 2))
            for i in range(NT):
                pool.indirect_dma_start(out=H[:, i, 0:2 * C], out_offset=None, in_=d_run1,
                                        in_offset=bass.IndirectOffsetOnAxis(ap=last_i[:, i:i + 1], axis=0)).then_inc(s_got1[i // GT], 16)

        @block.scalar
        def _(act):
            act.wait_ge(s_zeros, 1)
            flat = d_inj[0:EP, :].rearrange("(z p r) c -> z p (r c)", z=28, p=P)
            for z in range(28):
                act.dma_start(flat[z], zeros[:, :]).then_inc(s_injzero, 16)
            for n in range(3 * NT):
                i, (a, b) = n % NT, W_ORDER[n // NT]
                act.wait_ge(s_proj, n + 1)
                act.activation(H[:, i, a:b], bank[n % 2][0:NP, 0:b - a], ACT.Copy).then_inc(s_sel, 1)

            def exponents(s, r, c):
                act.wait_ge(diff_ready[s], r + 1)
                act.activation(expo[s][:, :, :, :], diff[s][:, :, :, :], ACT.Exp).then_inc(exps_ready[s], 1)

            def widen(s, r, c):
                act.wait_ge(prob_ready[s], r + 1)
                wait(act, probT[s], r)
                act.activation(prob_wide[s][:, :, :, :], prob[s][:, :, :, :].to_broadcast([P, TILES, 2, C]),
                               ACT.Copy).then_inc(wide_ready[s], 1)

            def copies(s, r, c):
                act.wait_ge(keep_in[s], 32 * (r + 1))
                wait(act, run_ready[s], r)
                act.activation(keep_late[s][:, :], keep[s][:, :], ACT.Copy).then_inc(keep_copied[s], 1)
                act.wait_ge(q2_ready[s], r + 1)
                wait(act, msg_ready[s], r)
                act.activation(q2_sb[s][:, :], q2[s], ACT.Copy).then_inc(q2_copied[s], 1)

            def store0(s, r, c):
                act.wait_ge(runT[s], r + 1)
                wait(act, stored[s], 16 * r)
                act.activation(stage0[s][:, :, :].rearrange("p j c -> p (j c)"), p_out0[:, :], ACT.Copy).then_inc(staged[s], 1)
                act.wait_ge(staged[s], r + 1)
                act.dma_start(d_run0[bass.ds(2 * CH * c, 2 * CH), :].rearrange("(p j h) c -> p j (h c)", j=TILES, h=2),
                              stage0[s][:, :, :]).then_inc(stored[s], 16)

            def step0(chunk):
                for work, d in ((exponents, -1), (copies, 0), (widen, -1), (store0, -2)):
                    if chunk(d):
                        work(*chunk(d))

            steps(act, step0, 0, 2)

            def square_and_root(g, first, source):
                act.wait_ge(s_square, first + g + 1)
                act.activation(sq[:, g * GT:(g + 1) * GT, :], source[:, g * GT:(g + 1) * GT, :], ACT.Square).then_inc(s_squared, 1)
                act.wait_ge(s_var, first + g + 1)
                act.activation(std[:, g * GT:(g + 1) * GT], var[:, g * GT:(g + 1) * GT], ACT.Sqrt).then_inc(s_sqrt, 1)

            for g in range(GROUPS):
                square_and_root(g, 0, acc)

            def messages(s, r, c):
                act.wait_ge(z_ready[s], r + 1)
                act.activation(relu[s][:, :], p_m[s][:, :], ACT.Relu).then_inc(relu_ready[s], 1)
                act.wait_ge(relu_ready[s], r + 1)
                wait(act, mexp_ready[s], r)
                act.activation(m[s][:, :], relu[s][:, :], ACT.Copy, bias=EPS).then_inc(m_ready[s], 1)

            def decays(s, r, c):
                act.wait_ge(y_ready[s], r + 1)
                act.activation(up[s], y[s][:, :], ACT.Relu).then_inc(updown_ready[s], 1)
                act.activation(down[s][:, :], y[s][:, :], ACT.Relu, scale=-1.0).then_inc(updown_ready[s], 1)
                wait(act, n_run[s], r)
                act.wait_ge(updown_ready[s], 2 * r + 2)
                act.activation(expm[s][:, :], down[s][:, :], ACT.Exp, scale=-1.0).then_inc(expm_ready[s], 1)
                act.activation(decay[s][:, :], up[s], ACT.Exp, scale=-1.0).then_inc(decay_ready[s], 1)

            def store_max(s, r, c):
                act.dma_start(d_max.rearrange("(c e) a -> c (e a)", c=C)[:, bass.ds(c * CH, CH)],
                              runmax[s][C:P, 1:CH + 1]).then_inc(max_out[s], 16)

            def store1(s, r, c):
                act.wait_ge(run1T[s], r + 1)
                wait(act, stored1[s], 16 * r)
                turned = p_out1[s][:, :].rearrange("p (j q h c) -> p j q h c", j=TILES, q=2, h=2)
                for q in range(2):
                    act.activation(stage1[s][:, :, :, q, :], turned[:, :, q], ACT.Copy).then_inc(staged1[s], 1)
                act.wait_ge(staged1[s], 2 * r + 2)
                act.dma_start(d_run1[bass.ds(2 * CH * c, 2 * CH), :].rearrange("(p j h) c -> p (j h c)", j=TILES, h=2),
                              stage1[s][:, :, :, :, :].rearrange("p j h q c -> p (j h q c)")).then_inc(stored1[s], 16)

            def step1(chunk):
                for work, d in ((decays, 0), (store_max, 0), (messages, 1), (store1, -1)):
                    if chunk(d):
                        work(*chunk(d))

            steps(act, step1, 1, 1)

            act.wait_ge(s_dmx, 1)
            act.activation(wgt[:, :, :], dmx[:, :, :], ACT.Exp).then_inc(s_wgt, 1)
            for g in range(GROUPS):
                for i in range(g * GT, (g + 1) * GT):
                    act.wait_ge(s_fT, i + 1)
                    if i >= 2:
                        act.wait_ge(s_y, i - 1)
                    act.activation(featsT[i % 2][0:C, :], bank[i % 2][0:C, 0:NP], ACT.Copy).then_inc(s_fTsb, 1)
                square_and_root(g, GROUPS, y_out)

        @block.tensor
        def _(pe):
            pe.wait_ge(s_nodes, 16 * 8)
            pe.wait_ge(s_typed, 2)
            for n in range(3 * NT):
                i, (a, b) = n % NT, W_ORDER[n // NT]
                if n >= 2:
                    pe.wait_ge(s_sel, n - 1)
                for k in range(2):
                    ins = pe.matmul(bank[n % 2][0:NP, 0:b - a], x_typed[k][:, i:N_NODES:NT], w_nodes[:, k, a:b],
                                    start=(k == 0), stop=(k == 1))
                ins.then_inc(s_proj, 1)
            pe.wait_ge(s_mbcol, 1)
            pe.matmul(bank[2][0:C, 0:1], ones[:, :], mb_col[:, :], start=True, stop=True).then_inc(s_mbps, 1)
            pe.wait_ge(s_const, 16 * 4)
            pe.wait_ge(s_weights, 16 * 10)
            pe.wait_ge(s_mb_i, 1)

            def project0(s, r, c):
                pe.wait_ge(masked[s], r + 1)
                wait(pe, prod_ready[s], r)
                pe.matmul(q4[s], w5[:, :], featm[s][:, :], start=True, stop=True)
                pe.wait_ge(got_rows[s], 16 * 2 * TILES * (r + 1))
                rows = [rows0[s][:, j, :, :].rearrange("p h c -> p (h c)") for j in range(TILES)]
                for j in range(TILES):
                    ins = pe.matmul(q4[s][:, j:CH:TILES], rows[j][:, 1:4 * C:2], ident[:, :], is_transpose=True,
                                    start=False, stop=True, skip_group_check=True)
                ins.then_inc(q4_ready[s], 1)
                wait(pe, q2_copied[s], r)
                pe.matmul(q2[s], w5[:, :], featm[s][:, :], start=True, stop=True)
                for j in range(TILES):
                    ins = pe.matmul(q2[s][:, j:CH:TILES], rows[j][:, 0:4 * C:2], ident[:, :], is_transpose=True,
                                    start=False, stop=True, skip_group_check=True)
                ins.then_inc(q2_ready[s], 1)
                pe.wait_ge(inj_in[s], 16 * (r + 1))
                if isinstance(c, int) and c == 0:
                    pe.wait_ge(s_sel, 3 * NT)
                else:
                    pe.wait_ge(h3_ready[1 - s], r + s)
                for j in range(TILES):
                    ins = pe.matmul(p_inj[:, j:CH:TILES], inj[s][:, j, :], ident[:, :], is_transpose=True,
                                    start=True, stop=True)
                ins.then_inc(injT[s], 1)

            def numerator(s, r, c):
                pe.wait_ge(prod_ready[s], r + 1)
                if not (isinstance(c, int) and c == 0):
                    pe.wait_ge(score_ready[1 - s], r + s)
                for j in range(TILES):
                    ins = pe.matmul(p_num[:, 2 * j:2 * j + 2], prod[s][:, j:CH:TILES], half_sum[:, :], start=True, stop=True)
                ins.then_inc(num_ready[s], 1)

            def turn_prob(s, r, c):
                pe.wait_ge(wide_ready[s], r + 1)
                if not (isinstance(c, int) and c == 0):
                    pe.wait_ge(msg_ready[1 - s], r + s)
                for j in range(TILES):
                    ins = pe.matmul(p_prob[:, j:CH:TILES], prob_wide[s][:, j, :, :].rearrange("p h c -> p (h c)"), ident[:, :],
                                    is_transpose=True, start=True, stop=True)
                ins.then_inc(probT[s], 1)

            def turn_run(s, r, c):
                pe.wait_ge(run_ready[s], r + 1)
                if not (isinstance(c, int) and c == 0):
                    pe.wait_ge(staged[1 - s], r + s)
                for j in range(TILES):
                    ins = pe.matmul(p_out0[:, j * P:(j + 1) * P], run[s][:, j:CH:TILES], ident[:, :], is_transpose=True,
                                    start=True, stop=True)
                ins.then_inc(runT[s], 1)

            def step0(chunk):
                for work, d in ((project0, 1), (numerator, 0), (turn_prob, -1), (turn_run, -2)):
                    if chunk(d):
                        work(*chunk(d))

            steps(pe, step0, 1, 2)

            def project1(s, r, c):
                pe.wait_ge(feat1_in[s], 32 * (r + 1))
                wait(pe, relu_ready[s], r)
                pe.matmul(p_m[s][:, :], we[:, :], feat[s][:, :], start=True, stop=True)
                pe.wait_ge(got1_rows[s], 16 * 2 * TILES * (r + 1))
                for j in range(TILES):
                    ins = pe.matmul(p_m[s][:, j:CH:TILES], rows1[s][:, j, :, :].rearrange("p h c -> p (h c)"), ident[:, :],
                                    is_transpose=True, start=False, stop=True, skip_group_check=True)
                ins.then_inc(z_ready[s], 1)

            def turn1(s, r, c):
                pe.wait_ge(n_run[s], r + 1)
                wait(pe, staged1[s], 2 * r)
                for j in range(TILES):
                    for q, src in enumerate((run_s[s], run_n[s])):
                        ins = pe.matmul(p_out1[s][:, (2 * j + q) * P:(2 * j + q + 1) * P], src[:, j:CH:TILES], ident[:, :],
                                        is_transpose=True, start=True, stop=True)
                ins.then_inc(run1T[s], 1)

            def step1(chunk):
                for work, d in ((project1, 1), (turn1, -1)):
                    if chunk(d):
                        work(*chunk(d))

            steps(pe, step1, 1, 1)

            pe.wait_ge(s_maxwide, 1)
            for b in range(2):
                ins = pe.matmul(bank[2][0:NP, b * C:(b + 1) * C], max_ab_wide[:, b, :], ident[0:C, 0:C],
                                start=True, stop=True)
            ins.then_inc(s_maxps, 1)
            for i in range(NT):
                pe.wait_ge(s_feats, i // GT + 1)
                if i >= 2:
                    pe.wait_ge(s_fTsb, i - 1)
                pe.matmul(bank[i % 2][0:C, 0:NP], acc[:, i, :], ident[0:NP, 0:NP], is_transpose=True,
                          start=True, stop=True).then_inc(s_fT, 1)
                pe.wait_ge(s_fTsb, i + 1)
                if i >= 2:
                    pe.wait_ge(s_ysum, i - 1)
                pe.matmul(wide[i % 2][0:NP, 0:C], featsT[i % 2][:, :], wm[:, :], start=True, stop=True).then_inc(s_y, 1)

        @block.vector
        def _(dve):
            linked = [0]

            def then(ins):
                linked[0] += 1
                ins.then_inc(s_vec, 1)
                dve.wait_ge(s_vec, linked[0])

            def nodes_of(ap):
                return ap.unsqueeze(2).to_broadcast([NP, ap.shape[1], C])

            def channels_of(ap, tiles=NT):
                return ap.unsqueeze(1).to_broadcast([NP, tiles, C])

            def edge_row(edge):
                then(dve.tensor_scalar(in_row[:, :], edge[:, :], float(HALF), float(1 - 2 * HALF), ALU.is_ge, ALU.mult))
                then(dve.scalar_tensor_tensor(tmp_n[:, :], edge[:, :], 2.0, in_row[:, :], ALU.mult, ALU.add))

            dve.memset(zeros[:, :], 0.0).then_inc(s_zeros, 1)
            then(dve.memset(xT[C:C + 1, :], 1.0))
            dve.wait_ge(s_nodes, 16 * 8)
            for k in range(2):
                dve.scalar_tensor_tensor(x_typed[k][:, :], ntype_i, float(k), xT[:, :], ALU.is_equal, ALU.mult).then_inc(s_typed, 1)
            dve.wait_ge(s_typed, 2)
            dve.wait_ge(s_iota, 2)
            dve.tensor_copy(lane[:, :], lane_i[:, :])
            then(dve.tensor_copy(node[:, :], node_i[:, :]))
            dve.wait_ge(s_keys, 32)
            then(dve.tensor_copy(keys16[:, :], keys[:, :]))
            for i in range(NT):
                ins = dve.tensor_scalar(le_rows[i % 4], keys16[:, :], node[:, i:i + 1], 0.0, ALU.is_le, ALU.add,
                                        accum_out=full_rows[:, i:i + 1])
                if i % 4 == 3 or i == NT - 1:
                    then(ins)
            dve.tensor_copy(row_i[:, :], full_rows[:, :]).then_inc(s_row_i, 1)
            dve.memset(w5[:, :], 0.0).then_inc(s_wzero, 1)
            dve.memset(we[:, :], 0.0).then_inc(s_wzero, 1)
            dve.memset(start[:, :], 0.0)
            for s in range(2):
                dve.memset(featsT[s][C:C + 1, :], 1.0)
                dve.memset(feat[s][:, :], 1.0)
            then(dve.memset(ones[:, :], 1.0))
            dve.memset(mb_col[:, :], 0.0).then_inc(s_ones, 1)
            dve.wait_ge(s_edges, 48)
            dve.tensor_tensor(keep_r[:, :], dst_i[:, :], prev_i[:, :], ALU.is_equal).then_inc(s_rowlists, 1)
            then(dve.tensor_tensor(dst_step[:, :], prev_i[:, :], dst_i[:, :], ALU.subtract))
            dve.tensor_scalar(pen_r[:, :], dst_step[:, :], BIG, None, ALU.mult).then_inc(s_rowlists, 1)
            dve.tensor_copy(type_r[:, :], type_i[:, :]).then_inc(s_rowlists, 1)
            then(dve.tensor_copy(mid[:, :], mid_i[:, :]))
            then(dve.tensor_tensor(mid_same[:, :], mid[:, 0:1], mid[:, 1:2], ALU.is_equal))
            then(dve.tensor_scalar(cross[:, :], node[:, :], mid[:, 1:2], mid_same[:, :], ALU.is_equal, ALU.mult))
            then(dve.tensor_scalar(not_cross[:, :], cross[:, :], -1.0, 1.0, ALU.mult, ALU.add))
            dve.wait_ge(s_found, 16 * NT)
            then(dve.tensor_tensor(le[:, :, :], found[:, :, :], node[:, :].unsqueeze(2).to_broadcast([NP, NT, P]), ALU.is_le))
            then(dve.tensor_reduce(in_row[:, :], le[:, :, :], AX.X, ALU.add))
            dve.scalar_tensor_tensor(end[:, :], full_rows[:, :], float(P), in_row[:, :], ALU.mult, ALU.add).then_inc(s_end, 1)
            dve.wait_ge(s_end, 1)
            then(dve.tensor_copy(start[:, 1:NT], end[:, 0:NT - 1]))
            then(dve.tensor_scalar(last[:, :], end[:, :], -1.0, 0.0, ALU.add, ALU.max))
            edge_row(last)
            dve.tensor_copy(last_i[:, :], tmp_n[:, :]).then_inc(s_last_i, 1)
            dve.wait_ge(s_last_i, 1)
            then(dve.scalar_tensor_tensor(tmp_n[:, :], last[:, :], float(-HALF), cross[:, :], ALU.add, ALU.mult))
            dve.tensor_reduce(mb_col[:, :], tmp_n[:, :], AX.X, ALU.add).then_inc(s_mbcol, 1)
            dve.wait_ge(s_mbcol, 1)
            dve.wait_ge(s_shift, 16)
            then(dve.tensor_tensor(has_edges[:, :], end[:, :], start[:, :], ALU.is_gt))
            edge_row(start)
            then(dve.tensor_tensor(tmp_n[:, :], tmp_n[:, :], has_edges[:, :], ALU.mult))
            then(dve.tensor_scalar(in_row[:, :], has_edges[:, :], -1.0, 1.0, ALU.mult, ALU.add))
            then(dve.scalar_tensor_tensor(in_row[:, :], node[:, :], float(DUMP), in_row[:, :], ALU.add, ALU.mult))
            then(dve.tensor_tensor(tmp_n[:, :], tmp_n[:, :], in_row[:, :], ALU.add))
            dve.tensor_copy(first_i[:, :], tmp_n[:, :]).then_inc(s_first_i, 1)
            dve.wait_ge(s_mbps, 1)
            dve.tensor_tensor(mb_i[:, :], bank[2][0:C, 0:1], lane[:, :], ALU.add).then_inc(s_mb_i, 1)

            for s in range(2):
                dve.memset(h3d[s][:, :], 0.0)
                then(dve.memset(run[s][:, :], 0.0))
            dve.wait_ge(s_const, 16 * 4)

            def score_parts(s, r, c):
                dve.wait_ge(num_ready[s], r + 1)
                dve.tensor_scalar(score[s][:, :, :, :].rearrange("p j h a -> p (j h a)"), p_num[:, 0:2 * TILES], 0.25, None,
                                  ALU.mult).then_inc(score_ready[s], 1)
                dve.wait_ge(score_ready[s], r + 1)
                dve.tensor_reduce(top[s][:, :, :], score[s][:, :, :, :], AX.X, ALU.max).then_inc(softmax_step[s], 1)
                dve.wait_ge(softmax_step[s], 3 * r + 1)
                wait(dve, exps_ready[s], r)
                dve.tensor_tensor(diff[s][:, :, :, :], score[s][:, :, :, :], top[s][:, :, :].unsqueeze(3), ALU.subtract).then_inc(diff_ready[s], 1)

            def mask(s, r, c):
                dve.wait_ge(feat_in[s], 16 * 4 * (r + 1))
                wait(dve, q2_ready[s], r)
                dve.scalar_tensor_tensor(featm[s][:, :], types[s][:, :], type_of_row[:, :], feat[s][:, :],
                                         ALU.is_equal, ALU.mult).then_inc(masked[s], 1)

            def products(s, r, c):
                dve.wait_ge(keep_in[s], 32 * (r + 1))
                dve.wait_ge(injT[s], r + 1)
                if not (isinstance(c, int) and c == 0):
                    dve.wait_ge(h3_ready[1 - s], r + s)
                dve.tensor_tensor_scan(h3d[s][:, :], keep[s][:, :], p_inj[:, :], h3d[1 - s][:, CH - 1:CH],
                                       ALU.mult, ALU.add).then_inc(h3_ready[s], 1)
                dve.wait_ge(h3_ready[s], r + 1)
                dve.wait_ge(q4_ready[s], r + 1)
                wait(dve, num_ready[s], r)
                dve.tensor_tensor(prod[s][:, :], h3d[s][:, :], q4[s], ALU.mult).then_inc(prod_ready[s], 1)

            def probabilities(s, r, c):
                dve.wait_ge(exps_ready[s], r + 1)
                dve.tensor_reduce(total[s][:, :, :], expo[s][:, :, :, :], AX.X, ALU.add).then_inc(softmax_step[s], 1)
                dve.wait_ge(softmax_step[s], 3 * r + 2)
                dve.reciprocal(inv[s][:, :, :], total[s][:, :, :]).then_inc(softmax_step[s], 1)
                dve.wait_ge(softmax_step[s], 3 * r + 3)
                wait(dve, wide_ready[s], r)
                dve.tensor_tensor(prob[s][:, :, :, :], expo[s][:, :, :, :], inv[s][:, :, :].unsqueeze(3), ALU.mult).then_inc(prob_ready[s], 1)

            def message_sums(s, r, c):
                dve.wait_ge(probT[s], r + 1)
                dve.wait_ge(q2_copied[s], r + 1)
                dve.tensor_tensor(msg[s][:, :], p_prob[:, :], q2_sb[s][:, :], ALU.mult).then_inc(msg_ready[s], 1)
                dve.wait_ge(msg_ready[s], r + 1)
                dve.wait_ge(keep_copied[s], r + 1)
                if not (isinstance(c, int) and c == 0):
                    dve.wait_ge(run_ready[1 - s], r + s)
                wait(dve, runT[s], r)
                dve.tensor_tensor_scan(run[s][:, :], keep_late[s][:, :], msg[s][:, :], run[1 - s][:, CH - 1:CH],
                                       ALU.mult, ALU.add).then_inc(run_ready[s], 1)

            def step0(chunk):
                for work, d in ((score_parts, -1), (mask, 1), (products, 0), (probabilities, -1), (message_sums, -2)):
                    if chunk(d):
                        work(*chunk(d))

            steps(dve, step0, 1, 2)

            def layer_norm(src, g, first):
                at = slice(g * GT, (g + 1) * GT)
                then(dve.tensor_reduce(mean[:, at], src[:, at, :], AX.X, ALU.add))
                then(dve.tensor_scalar(mean[:, at], mean[:, at], 1.0 / C, None, ALU.mult))
                dve.tensor_tensor(src[:, at, :], src[:, at, :], nodes_of(mean[:, at]), ALU.subtract).then_inc(s_square, 1)
                dve.wait_ge(s_squared, first + g + 1)
                then(dve.tensor_reduce(var[:, at], sq[:, at, :], AX.X, ALU.add))
                dve.tensor_scalar(var[:, at], var[:, at], 1.0 / C, LN_EPS, ALU.mult, ALU.add).then_inc(s_var, 1)
                dve.wait_ge(s_sqrt, first + g + 1)
                then(dve.reciprocal(rstd[:, at], std[:, at]))
                return dve.tensor_tensor(x1[:, at, :], src[:, at, :], nodes_of(rstd[:, at]), ALU.mult)

            for s in range(2):
                dve.memset(feat[s][:, :], 1.0)
                dve.memset(run_s[s][:, :], 0.0)
                dve.memset(run_n[s][:, :], 0.0)
                then(dve.memset(runmax[s][:, :], 0.0))
            dve.wait_ge(s_sel, 3 * NT)
            then(dve.tensor_tensor(acc[:, :, :], x_sb[:, :, :], H[:, :, 0:C], ALU.add))
            dve.wait_ge(s_cut0, 16)
            then(dve.tensor_tensor(y_out, channels_of(cut0[:, :]), nodes_of(cross[:, :]), ALU.mult))
            dve.tensor_tensor(acc[:, :, :], acc[:, :, :], y_out, ALU.add).then_inc(s_ones1, 1)
            dve.wait_ge(s_ones1, 1)
            for g in range(GROUPS):
                at = slice(g * GT, (g + 1) * GT)
                dve.wait_ge(s_got0[g], 16 * GT)
                then(dve.tensor_tensor(got0[:, at, :], got0[:, at, :], nodes_of(has_edges[:, at]), ALU.mult))
                then(dve.tensor_tensor(acc[:, at, :], acc[:, at, :], got0[:, at, :], ALU.add))
                layer_norm(acc, g, 0).then_inc(s_x1, 1)
            dve.wait_ge(s_x1, GROUPS)

            def maxima(s, r, c):
                first = isinstance(c, int) and c == 0
                wait(dve, max_out[s], 16 * r)
                if not first:
                    dve.wait_ge(max_ready[1 - s], 2 * (r + s))
                dve.tensor_copy(runmax[s][:, 0:1], runmax[1 - s][:, CH:CH + 1]).then_inc(max_ready[s], 1)
                dve.wait_ge(pen_in[s], 32 * (r + 1))
                dve.wait_ge(m_ready[s], r + 1)
                dve.tensor_tensor_scan(runmax[s][:, 1:CH + 1], keep[s][:, :], m[s][:, :], runmax[1 - s][:, CH:CH + 1],
                                       ALU.add, ALU.max).then_inc(max_ready[s], 1)
                dve.wait_ge(max_ready[s], 2 * r + 2)
                wait(dve, updown_ready[s], 2 * r)
                dve.tensor_tensor(y[s][:, :], runmax[s][:, 0:CH], keep[s][:, :], ALU.add).then_inc(shift_ready[s], 1)
                dve.wait_ge(shift_ready[s], r + 1)
                dve.tensor_tensor(y[s][:, :], m[s][:, :], y[s][:, :], ALU.subtract).then_inc(y_ready[s], 1)

            def sums(s, r, c):
                first = isinstance(c, int) and c == 0
                dve.wait_ge(expm_ready[s], r + 1)
                dve.tensor_tensor(mexp[s][:, :], m[s][:, :], expm[s][:, :], ALU.mult).then_inc(mexp_ready[s], 1)
                dve.wait_ge(decay_ready[s], r + 1)
                wait(dve, run1T[s], r)
                if not first:
                    dve.wait_ge(s_run[1 - s], r + s)
                dve.tensor_tensor_scan(run_s[s][:, :], decay[s][:, :], expm[s][:, :], run_s[1 - s][:, CH - 1:CH],
                                       ALU.mult, ALU.add).then_inc(s_run[s], 1)
                dve.wait_ge(mexp_ready[s], r + 1)
                if not first:
                    dve.wait_ge(n_run[1 - s], r + s)
                dve.tensor_tensor_scan(run_n[s][:, :], decay[s][:, :], mexp[s][:, :], run_n[1 - s][:, CH - 1:CH],
                                       ALU.mult, ALU.add).then_inc(n_run[s], 1)

            def step1(chunk):
                for work, d in ((maxima, 0), (sums, -1)):
                    if chunk(d):
                        work(*chunk(d))

            steps(dve, step1, 0, 1)

            dve.wait_ge(s_mb, 16)
            then(dve.tensor_copy(max_ab[:, 0:1], runmax[1][0:C, CH:CH + 1]))
            dve.tensor_copy(max_ab_wide[:, :, :], max_ab[:, :].unsqueeze(2).to_broadcast([C, 2, NP])).then_inc(s_maxwide, 1)
            dve.wait_ge(s_maxps, 1)
            then(dve.tensor_copy(mx[:, :, :], bank[2][0:NP, 0:2 * C].rearrange("p (q c) -> p q c", q=2)))
            then(dve.tensor_tensor(mm[:, :], mx[:, 0, :], mx[:, 1, :], ALU.max))
            dve.tensor_tensor(dmx[:, :, :], mx[:, :, :], mm[:, :].unsqueeze(1).to_broadcast([NP, 2, C]), ALU.subtract).then_inc(s_dmx, 1)
            dve.wait_ge(s_wgt, 1)
            dve.wait_ge(s_cut1, 16)
            then(dve.tensor_tensor(scale_b, channels_of(wgt[:, 1, :]), nodes_of(cross[:, :]), ALU.mult))
            then(dve.tensor_tensor(scale_b, scale_b, nodes_of(not_cross[:, :]), ALU.add))
            then(dve.tensor_tensor(cut1[:, :, :], cut1[:, :, :], wgt[:, 0:1, :].to_broadcast([NP, 2, C]), ALU.mult))
            for q, part in ((0, acc), (1, got0)):
                then(dve.tensor_tensor(part[:, :, :], channels_of(cut1[:, q, :]), nodes_of(cross[:, :]), ALU.mult))
            for g in range(GROUPS):
                at = slice(g * GT, (g + 1) * GT)
                dve.wait_ge(s_got1[g], 16 * GT)
                for q, part in ((0, acc), (1, got0)):
                    then(dve.tensor_tensor(got1[:, at, q, :], got1[:, at, q, :], scale_b[:, at, :], ALU.mult))
                    then(dve.tensor_tensor(part[:, at, :], got1[:, at, q, :], part[:, at, :], ALU.add))
                then(dve.reciprocal(acc[:, at, :], acc[:, at, :]))
                then(dve.tensor_tensor(got0[:, at, :], got0[:, at, :], acc[:, at, :], ALU.mult))
                then(dve.tensor_tensor(got0[:, at, :], got0[:, at, :], nodes_of(has_edges[:, at]), ALU.mult))
                dve.tensor_tensor(acc[:, at, :], x1[:, at, :], got0[:, at, :], ALU.add).then_inc(s_feats, 1)
            for g in range(GROUPS):
                for i in range(g * GT, (g + 1) * GT):
                    dve.wait_ge(s_y, i + 1)
                    dve.tensor_tensor(y_out[:, i, :], wide[i % 2][0:NP, 0:C], x1[:, i, :], ALU.add).then_inc(s_ysum, 1)
                dve.wait_ge(s_ysum, (g + 1) * GT)
                layer_norm(y_out, g, GROUPS).then_inc(s_fin, 1)


def kernel(x, src, dst, edge_attr_16, edge_attr_32, edge_type_3, node_type_2,
           L0_gnn_W1, L0_gnn_b1, L0_gnn_W2, L0_gnn_b2, L0_gnn_W3, L0_gnn_b3, L0_gnn_W4, L0_gnn_b4,
           L0_gnn_W5, L0_gnn_b5, L1_gnn_We, L1_gnn_be, L1_gnn_Wm, L1_gnn_bm):
    import numpy as np
    import concourse.bacc as bacc
    from concourse.bass_utils import run_bass_kernel_spmd as run

    def padded(a, value):
        return np.concatenate([np.asarray(a), np.full(EP - N_EDGES, value, np.int32)])

    def features(a):
        a = np.asarray(a).T
        return np.concatenate([a, np.zeros((a.shape[0], EP - N_EDGES), a.dtype)], axis=1)

    dst_p = padded(dst, N_NODES)
    src_p = padded(src, 0)
    row = np.arange(P) % C
    type_of_row = np.where(row < T_EDGE * F0, row // F0, np.where(row < T_EDGE * (F0 + 1), row - T_EDGE * F0, -1))
    arrays = {
        "x": x, "xT": np.asarray(x).T,
        "src": src_p.reshape(2, CHUNKS, P, TILES).transpose(1, 2, 0, 3).reshape(CHUNKS * P, 2 * TILES),
        "dst": dst_p.reshape(ROWS, P),
        "dst_prev": np.concatenate([np.full(1, -1, np.int32), dst_p[:-1]]).reshape(P, ROWS),
        "keys": dst_p[P - 1::P].reshape(1, ROWS),
        "mid": dst_p[HALF - 1:HALF + 1].reshape(1, 2),
        "etype": padded(edge_type_3, 0).reshape(P, ROWS),
        "node_type": np.asarray(node_type_2).reshape(1, N_NODES),
        "ea16x3T": np.concatenate([features(edge_attr_16)] * T_EDGE), "ea32T": features(edge_attr_32),
        "W1": L0_gnn_W1, "b1": L0_gnn_b1, "W3": L0_gnn_W3, "b3": L0_gnn_b3,
        "W24": np.stack([L0_gnn_W2, L0_gnn_W4], axis=-1).reshape(2, C, 2 * C),
        "b24": np.stack([L0_gnn_b2, L0_gnn_b4], axis=-1).reshape(2, 2 * C),
        "W5": L0_gnn_W5, "b5": L0_gnn_b5,
        "We": L1_gnn_We, "be": np.asarray(L1_gnn_be).reshape(1, C),
        "Wm": L1_gnn_Wm, "bm": np.asarray(L1_gnn_bm).reshape(1, C),
        "ident": np.eye(P, dtype=np.float32),
        "half_sum": np.kron(np.eye(2), np.ones((C, 1))).astype(np.float32),
        "type_of_row": type_of_row.astype(np.float32).reshape(P, 1),
    }
    nc = bacc.Bacc("TRN2", target_bir_lowering=False, num_devices=1)
    feed, aps = {}, {}
    for name, a in arrays.items():
        a = np.ascontiguousarray(a)
        feed[f"in_{name}"] = a
        aps[name] = nc.dram_tensor(f"in_{name}", a.shape, mybir.dt.from_np(a.dtype), kind="ExternalInput").ap()
    out = nc.dram_tensor("out", (N_NODES, C), mybir.dt.float32, kind="ExternalOutput").ap()
    gnn_program(nc, aps, out)
    return run(nc, [feed], core_ids=[0]).results[0]["out"]
```

```python
import concourse.bass as bass
from concourse import mybir
from contextlib import ExitStack

N_NODES = 3125
N_EDGES = 100000
C = 64
F0, F1 = 16, 32
T_EDGE = 3
P = 128
NP = 125
NT = N_NODES // NP
CH = 512
TILES = CH // P
CHUNKS = 2 * -(-N_EDGES // (4 * CH))
HALF = CHUNKS * CH
EP = 2 * HALF
ROW = 256
ROWS = EP // ROW
PER_P = EP // P
CUT_ROW = 2 * (HALF - 1)
DUMP = EP
EPS = 1e-7
LN_EPS = 1e-5
GROUPS = 5
GT = NT // GROUPS
NT_DVE = 12
W_ORDER = ((C, 3 * C), (3 * C, 4 * C), (0, C))
BIG = 1e30


def gnn_program(nc, t, out):
    f32, bf16, i32 = mybir.dt.float32, mybir.dt.bfloat16, mybir.dt.int32
    ALU, ACT, AX = mybir.AluOpType, mybir.ActivationFunctionType, mybir.AxisListType
    ctx = ExitStack()
    with ctx:
        def sb(name, shape, dt=f32):
            return ctx.enter_context(nc.sbuf_tensor(name, shape, dt))

        def pb(name, cols):
            return ctx.enter_context(nc.psum_tensor(name, [P, cols], f32))

        def sem(name):
            return ctx.enter_context(nc.semaphore(name))

        def sems(name):
            return [sem(f"{name}_{s}") for s in range(2)]

        def scratch(name, shape, dt=f32):
            return nc.dram_tensor(name, shape, dt).ap()

        d_keep = scratch("d_keep", [1, EP], bf16)
        d_pen = scratch("d_pen", [1, EP], bf16)
        d_type = scratch("d_type", [1, EP], bf16)
        d_h24 = scratch("d_h24", [N_NODES, 2 * C])
        d_h3 = scratch("d_h3", [N_NODES, C])
        d_inj = scratch("d_inj", [EP + NP * NT, C])
        d_run0 = scratch("d_run0", [EP, C])
        d_x1 = scratch("d_x1", [N_NODES, C])
        d_run1 = scratch("d_run1", [EP, 2 * C])
        d_max = scratch("d_max", [C * HALF, 1])

        ident = sb("ident", [P, P])
        half_sum = sb("half_sum", [P, 2])
        type_of_row = sb("type_of_row", [P, 1])
        ones = sb("ones", [NP, C])
        zeros = sb("zeros", [P, 1792])
        w_nodes = sb("w_nodes", [C + 1, 2, 4 * C])
        w5 = sb("w5", [P, P])
        we = sb("we", [P, P])
        wm = sb("wm", [C + 1, C])
        late = sb("late", [NP, NT, 2, C])
        xT = late[0:C + 1, :, :, :].rearrange("p i q c -> p (i q c)")[:, 0:N_NODES]
        typed = [sb(f"typed{k}", [NP, 2, NT, C]) for k in range(2)]
        x_typed = [b[0:C + 1, :, :, :].rearrange("p a i c -> p (a i c)")[:, 0:N_NODES]
                   for b in typed]
        x_sb = sb("x_sb", [NP, NT, C])
        H = sb("H", [NP, NT, 4 * C])
        node_i = sb("node_i", [NP, NT], i32)
        node = sb("node", [NP, NT])
        keys = sb("keys", [NP, ROWS], i32)
        full_rows = sb("full_rows", [NP, NT])
        row_i = sb("row_i", [NP, NT], i32)
        block1 = sb("block1", [P, NT * ROW])
        found = block1[0:NP, :].bitcast(i32).rearrange("p (i k) -> p i k", i=NT)
        ntype_i = sb("ntype_i", [C + 1, N_NODES], i32)
        le = [sb(f"le{k}", [NP, ROWS], bf16) for k in range(4)]
        sign = [sb(f"sign{k}", [NP, ROWS], bf16) for k in range(2)]
        node_half = sb("node_half", [NP, NT])
        in_row = sb("in_row", [NP, NT])
        end = sb("end", [NP, NT])
        start = sb("start", [NP, NT])
        has_edges = sb("has_edges", [NP, NT])
        last = sb("last", [NP, NT])
        last_i = sb("last_i", [NP, NT], i32)
        tmp_n = sb("tmp_n", [NP, NT])
        first_i = sb("first_i", [NP, NT], i32)
        mid_i = sb("mid_i", [NP, 2], i32)
        mid = sb("mid", [NP, 2])
        mid_same = sb("mid_same", [NP, 1])
        cross = sb("cross", [NP, NT])
        not_cross = sb("not_cross", [NP, NT])
        fix = sb("fix", [16, C])
        mb_col = sb("mb_col", [NP, 1])
        lane_i = sb("lane_i", [C, 1], i32)
        lane = sb("lane", [C, 1])
        mb_i = sb("mb_i", [C, 1], i32)
        max_ab = sb("max_ab", [C, 2])
        max_ab_wide = sb("max_ab_wide", [C, 2, NP])
        dst_i = sb("dst_i", [P, PER_P], i32)
        prev_i = sb("prev_i", [P, PER_P], i32)
        type_i = sb("type_i", [P, PER_P], i32)
        dst_step = sb("dst_step", [P, PER_P])
        keep_r = sb("keep_r", [P, PER_P], bf16)
        pen_r = sb("pen_r", [P, PER_P], bf16)
        type_r = sb("type_r", [P, PER_P], bf16)
        idx = [sb(f"idx{s}", [P, 2 * TILES], i32) for s in range(2)]
        rows0 = [sb(f"rows0_{s}", [P, TILES, 2, 2 * C]) for s in range(2)]
        rows1 = [r[:, :, :, :].rearrange("p j h c -> p (j h c)")[:, 0:TILES * 2 * C].rearrange("p (j h c) -> p j h c", j=TILES, h=2)
                 for r in rows0]
        types = [sb(f"types{s}", [P, CH], bf16) for s in range(2)]
        feat = [sb(f"feat{s}", [P, CH]) for s in range(2)]
        featm = [sb(f"featm{s}", [P, CH]) for s in range(2)]
        keep = [sb(f"keep{s}", [P, CH], bf16) for s in range(2)]
        inj = [sb(f"inj{s}", [P, TILES, 2 * C]) for s in range(2)]
        keep_late = [sb(f"keep_late{s}", [P, CH], bf16) for s in range(2)]
        h3d = [sb(f"h3d{s}", [P, CH]) for s in range(2)]
        prod = [sb(f"prod{s}", [P, CH]) for s in range(2)]
        q2_sb = [sb(f"q2_sb{s}", [P, CH]) for s in range(2)]
        prob_wide = [sb(f"prob_wide{s}", [P, TILES, 2, C]) for s in range(2)]
        msg = [sb(f"msg{s}", [P, CH]) for s in range(2)]
        run = [sb(f"run{s}", [P, CH]) for s in range(2)]
        score, diff, expo, prob = ([sb(f"{n}{s}", [P, TILES, 2, 1]) for s in range(2)] for n in ("score", "diff", "expo", "prob"))
        top, total, inv = ([sb(f"{n}{s}", [P, TILES, 2]) for s in range(2)] for n in ("top", "total", "inv"))
        stage0 = [sb(f"stage0_{s}", [P, TILES, 2 * C]) for s in range(2)]
        relu, m, y, down, mexp = prod, h3d, q2_sb, msg, run
        up = [w[:, :, :, :].rearrange("p j h c -> p (j h c)") for w in prob_wide]
        decay = featm
        taken = [0]

        def carve(cols):
            taken[0] += cols
            return block1[:, taken[0] - cols:taken[0]]

        expm, run_s, run_n = ([carve(CH) for s in range(2)] for _ in range(3))
        stage1 = [carve(TILES * 4 * C).rearrange("p (j h q c) -> p j h q c", j=TILES, h=2, q=2) for s in range(2)]
        runmax = [carve(CH + 1) for s in range(2)]
        acc, x1 = (typed[0][:, a, :, :] for a in range(2))
        got0, across = typed[1][:, 0, :, :], typed[1][:, 1, :, :]
        far_part = typed[1][:, :, :, :].rearrange("p a i c -> p (a i c)").rearrange("p (i q c) -> p i q c", q=2, c=C)
        sq, centred = H[:, :, 2 * C:3 * C], H[:, :, 3 * C:4 * C]
        cut0 = sb("cut0", [NP, C])
        mean = sb("mean", [NP, NT])
        var = sb("var", [NP, NT])
        std = sb("std", [NP, NT])
        rstd = sb("rstd", [NP, NT])
        got1 = H[:, :, 0:2 * C].rearrange("p i (q c) -> p i q c", q=2)
        cut1 = sb("cut1", [NP, 2, C])
        mx = sb("mx", [NP, 2, C])
        mm = sb("mm", [NP, C])
        dmx = sb("dmx", [NP, 2, C])
        wgt = sb("wgt", [NP, 2, C])
        featsT = [sb(f"featsT{s}", [C + 1, NP]) for s in range(2)]

        wide = [pb(f"wide{s}", 2 * CH) for s in range(2)]
        bank = [pb(f"bank{b}", CH) for b in range(4)]
        q2 = [w[:, 0:CH] for w in wide]
        q4 = [w[:, CH:2 * CH] for w in wide]
        p_inj, p_num, p_prob, p_out0 = bank
        p_m, p_out1 = bank[0:2], wide

        s_const, s_nodes, s_edges = sem("s_const"), sem("s_nodes"), sem("s_edges")
        s_wzero, s_weights, s_ones = sem("s_wzero"), sem("s_weights"), sem("s_ones")
        s_keys, s_iota, s_zeros = sem("s_keys"), sem("s_iota"), sem("s_zeros")
        s_half, s_signs = sem("s_half"), sem("s_signs")
        s_typed, s_proj, s_sel = sem("s_typed"), sem("s_proj"), sem("s_sel")
        s_h24, s_h3, s_rowlists, s_lists = sem("s_h24"), sem("s_h3"), sem("s_rowlists"), sem("s_lists")
        s_row_i, s_found, s_end, s_shift = sem("s_row_i"), [sem(f"s_found_{g}") for g in range(GROUPS)], sem("s_end"), sem("s_shift")
        s_first_i, s_last_i, s_injzero, s_inj = sem("s_first_i"), sem("s_last_i"), sem("s_injzero"), sem("s_inj")
        s_fix, s_fixed, s_mbcol, s_mbps, s_mb_i = sem("s_fix"), sem("s_fixed"), sem("s_mbcol"), sem("s_mbps"), sem("s_mb_i")
        s_vec = sem("s_vec")
        s_chunks = sem("s_chunks")
        idx_in, got_rows, feat_in, keep_in, inj_in = sems("idx_in"), sems("got_rows"), sems("feat_in"), sems("keep_in"), sems("inj_in")
        masked, q4_ready, q2_ready, injT = sems("masked"), sems("q4_ready"), sems("q2_ready"), sems("injT")
        keep_copied, q2_copied, h3_ready, prod_ready = sems("keep_copied"), sems("q2_copied"), sems("h3_ready"), sems("prod_ready")
        num_ready, score_ready, diff_ready = sems("num_ready"), sems("score_ready"), sems("diff_ready")
        exps_ready, prob_ready = sems("exps_ready"), sems("prob_ready")
        softmax_step = sems("softmax_step")
        wide_ready, probT, msg_ready = sems("wide_ready"), sems("probT"), sems("msg_ready")
        run_ready, runT, staged, stored = sems("run_ready"), sems("runT"), sems("staged"), sems("stored")
        s_cut0, s_square, s_squared, s_var, s_sqrt, s_x1, s_x1_out = (sem("s_cut0"), sem("s_square"), sem("s_squared"),
                                                                      sem("s_var"), sem("s_sqrt"), sem("s_x1"), sem("s_x1_out"))
        s_got = [sem(f"s_got_{g}") for g in range(GROUPS)]
        idx1_in, got1_rows, feat1_in, pen_in = sems("idx1_in"), sems("got1_rows"), sems("feat1_in"), sems("pen_in")
        z_ready, relu_ready, m_ready = sems("z_ready"), sems("relu_ready"), sems("m_ready")
        max_ready = sems("max_ready")
        shift_ready, y_ready = sems("shift_ready"), sems("y_ready")
        updown_ready, decay_ready, expm_ready = sems("updown_ready"), sems("decay_ready"), sems("expm_ready")
        mexp_ready, s_run, n_run, run1T, staged1, stored1, max_out = (sems("mexp_ready"), sems("s_run"), sems("n_run"),
                                                                     sems("run1T"), sems("staged1"), sems("stored1"), sems("max_out"))
        s_ones1 = sem("s_ones1")
        s_cut1, s_mb, s_maxwide, s_maxps, s_dmx, s_wgt = (sem("s_cut1"), sem("s_mb"), sem("s_maxwide"),
                                                                  sem("s_maxps"), sem("s_dmx"), sem("s_wgt"))
        s_feats, s_fT, s_fTsb, s_y, s_fin, s_out = (sem("s_feats"), sem("s_fT"), sem("s_fTsb"), sem("s_y"),
                                                       sem("s_fin"), sem("s_out"))

        block = ctx.enter_context(nc.Block())

        PEELED = 4

        def peeled(c):
            return (c % 2, c // 2, c) if 0 <= c < CHUNKS else None

        def steps(eng, step, before, after, first=PEELED):
            for c in range(-before, first):
                step(lambda d: peeled(c + d))
            stop = CHUNKS - after - (CHUNKS - after) % 2
            with eng.Fori(first // 2, stop // 2) as i:
                for k in range(2):
                    step(lambda d: ((k + d) % 2, i + (k + d) // 2, 2 * i + k + d))
            for c in range(stop, CHUNKS + after):
                step(lambda d: peeled(c + d))

        def wait(eng, semaphore, count):
            if not (isinstance(count, int) and count == 0):
                eng.wait_ge(semaphore, count)

        @block.sync
        def _(sp):
            sp.dma_start(ntype_i[:, :], t["node_type"].to_broadcast([C + 1, N_NODES])).then_inc(s_nodes, 16)
            sp.dma_start(xT[0:C], t["xT"]).then_inc(s_nodes, 16)
            sp.dma_start(keys[:, :], t["keys"].to_broadcast([NP, ROWS])).then_inc(s_keys, 16)
            sp.dma_start(mid_i[:, :], t["mid"].to_broadcast([NP, 2])).then_inc(s_keys, 16)
            for name, a, b in (("24", C, 3 * C), ("3", 3 * C, 4 * C), ("1", 0, C)):
                sp.dma_start(w_nodes[0:C, :, a:b], t["W" + name].rearrange("t f h -> f t h")).then_inc(s_nodes, 16)
                sp.dma_start(w_nodes[C:C + 1, :, a:b], t["b" + name].rearrange("(a t) h -> a t h", a=1)).then_inc(s_nodes, 16)
            sp.dma_start(dst_i[:, :], t["dst"].rearrange("a b -> (a b)").rearrange("(p k) -> p k", p=P)).then_inc(s_edges, 16)
            sp.dma_start(prev_i[:, :], t["dst_prev"]).then_inc(s_edges, 16)
            sp.dma_start(type_i[:, :], t["etype"]).then_inc(s_edges, 16)
            sp.dma_start(ident[:, :], t["ident"]).then_inc(s_const, 16)
            sp.dma_start(half_sum[:, :], t["half_sum"]).then_inc(s_const, 16)
            sp.dma_start(type_of_row[:, :], t["type_of_row"]).then_inc(s_const, 16)
            sp.dma_start(x_sb[:, :, :], t["x"].rearrange("(p i) c -> p i c", i=NT)).then_inc(s_const, 16)
            def offsets(c):
                return sp.snap(c * P), sp.snap(c * (2 * CH)), [sp.snap(c * CH), sp.snap(c * CH + HALF)]

            def load_src(s, r, of_src, used_up, landed):
                wait(sp, used_up[s], 16 * 2 * TILES * r)
                sp.dma_start(idx[s][:, :], t["src"][bass.ds(of_src, P), :]).then_inc(landed[s], 16)

            def load_features0(s, r, of_edge):
                wait(sp, masked[s], r)
                for h in range(2):
                    sp.dma_start(types[s][h * C:(h + 1) * C, :],
                                 d_type[:, bass.ds(of_edge[h], CH)].to_broadcast([C, CH])).then_inc(feat_in[s], 16)
                    sp.dma_start(feat[s][h * C:h * C + T_EDGE * F0, :],
                                 t["ea16x3T"][:, bass.ds(of_edge[h], CH)]).then_inc(feat_in[s], 16)

            def load_keep(s, r, of_edge):
                wait(sp, keep_copied[s], r)
                wait(sp, h3_ready[s], r)
                for h in range(2):
                    sp.dma_start(keep[s][h * C:(h + 1) * C, :],
                                 d_keep[:, bass.ds(of_edge[h], CH)].to_broadcast([C, CH])).then_inc(keep_in[s], 16)

            def load_inj(s, r, of_inj):
                wait(sp, injT[s], r)
                sp.dma_start(inj[s][:, :, :], d_inj[bass.ds(of_inj, 2 * CH), :]
                             .rearrange("(p j h) c -> p j (h c)", j=TILES, h=2)).then_inc(inj_in[s], 16)

            for s in range(2):
                load_src(s, 0, s * P, got_rows, idx_in)
            sp.wait_ge(s_wzero, 2)
            for h in range(2):
                b = h * C
                sp.dma_start(w5[b:b + T_EDGE * F0, b:b + C], t["W5"].rearrange("t f h -> (t f) h")).then_inc(s_weights, 16)
                sp.dma_start(w5[b + T_EDGE * F0:b + T_EDGE * (F0 + 1), b:b + C], t["b5"]).then_inc(s_weights, 16)
            sp.wait_ge(s_sel, NT)
            sp.dma_start(d_h24.rearrange("(p i) c -> p i c", i=NT), H[:, :, C:3 * C]).then_inc(s_h24, 16)
            sp.wait_ge(s_rowlists, 3)
            for dst, src in ((d_keep, keep_r), (d_pen, pen_r), (d_type, type_r)):
                sp.dma_start(dst.rearrange("a (p b) -> (a p) b", p=P), src[:, :]).then_inc(s_lists, 16)
            for h in range(2):
                b = h * C
                sp.dma_start(we[b:b + F1, b:b + C], t["We"]).then_inc(s_weights, 16)
                sp.dma_start(we[b + F1:b + F1 + 1, b:b + C], t["be"]).then_inc(s_weights, 16)
            sp.dma_start(wm[0:C, :], t["Wm"]).then_inc(s_weights, 16)
            sp.dma_start(wm[C:C + 1, :], t["bm"]).then_inc(s_weights, 16)
            sp.wait_ge(s_sel, 2 * NT)
            sp.dma_start(d_h3.rearrange("(p i) c -> p i c", i=NT), H[:, :, 3 * C:4 * C]).then_inc(s_h3, 16)
            sp.wait_ge(s_lists, 48)
            sp.wait_ge(s_ones, 5)
            for s in range(2):
                load_features0(s, 0, [s * CH, s * CH + HALF])
                load_keep(s, 0, [s * CH, s * CH + HALF])
            sp.wait_ge(s_end, 1)
            sp.dma_start(start[1:NP, 0:1], end[0:NP - 1, NT - 1:NT]).then_inc(s_shift, 16)
            sp.wait_ge(s_fix, 16)
            sp.wait_ge(s_inj, 16 * NT)
            sp.dma_start(d_inj[1:2, :], fix[0:1, :]).then_inc(s_fixed, 16)
            sp.wait_ge(s_fixed, 16)
            for s in range(2):
                load_inj(s, 0, s * (2 * CH))

            with sp.Fori(1, CHUNKS // 2) as i:
                for s in range(2):
                    of_src, of_inj, of_edge = offsets(2 * i + s)
                    load_src(s, i, of_src, got_rows, idx_in)
                    load_features0(s, i, of_edge)
                    load_inj(s, i, of_inj)
                    load_keep(s, i, of_edge)

            for s in range(2):
                sp.wait_ge(stored[s], 16 * (CHUNKS // 2))
            sp.dma_start(cut0[:, :], d_run0[CUT_ROW:CUT_ROW + 1, :].to_broadcast([NP, C])).then_inc(s_cut0, 16)

            def load_features1(s, r, of_edge):
                wait(sp, z_ready[s], r)
                for h in range(2):
                    sp.dma_start(feat[s][h * C:h * C + F1, :],
                                 t["ea32T"][:, bass.ds(of_edge[h], CH)]).then_inc(feat1_in[s], 16)

            def load_pen(s, r, of_edge):
                sp.wait_ge(s_lists, 48)
                wait(sp, shift_ready[s], r)
                for h in range(2):
                    sp.dma_start(keep[s][h * C:(h + 1) * C, :],
                                 d_pen[:, bass.ds(of_edge[h], CH)].to_broadcast([C, CH])).then_inc(pen_in[s], 16)

            sp.wait_ge(s_ones1, 1)
            for s in range(2):
                sp.wait_ge(got_rows[s], 16 * 2 * TILES * (CHUNKS // 2))
                sp.dma_start(idx[s][:, :], t["src"][s * P:(s + 1) * P, :]).then_inc(idx1_in[s], 16)
                load_features1(s, 0, [s * CH, s * CH + HALF])
                load_pen(s, 0, [s * CH, s * CH + HALF])
            for g in range(GROUPS):
                sp.wait_ge(s_x1, g + 1)
                sp.dma_start(d_x1.rearrange("(p i) c -> p i c", i=NT)[:, g * GT:(g + 1) * GT, :],
                             x1[:, g * GT:(g + 1) * GT, :]).then_inc(s_x1_out, 16)
            with sp.Fori(1, CHUNKS // 2) as i:
                for s in range(2):
                    of_src, _, of_edge = offsets(2 * i + s)
                    load_src(s, i, of_src, got1_rows, idx1_in)
                    load_features1(s, i, of_edge)
                    load_pen(s, i, of_edge)

            for s in range(2):
                sp.wait_ge(stored1[s], 16 * (CHUNKS // 2))
            sp.dma_start(cut1[:, :, :], d_run1[CUT_ROW:CUT_ROW + 1, :].rearrange("a (q c) -> a q c", q=2).to_broadcast([NP, 2, C])).then_inc(s_cut1, 16)
            for g in range(GROUPS):
                sp.wait_ge(s_fin, g + 1)
                sp.dma_start(out.rearrange("(p i) c -> p i c", i=NT)[:, g * GT:(g + 1) * GT, :],
                             x1[:, g * GT:(g + 1) * GT, :]).then_inc(s_out, 16)
            sp.wait_ge(s_out, 16 * GROUPS)

        @block.gpsimd
        def _(pool):
            pool.iota(node_i[:, :], pattern=[[1, NT]], base=0, channel_multiplier=NT).then_inc(s_iota, 1)
            pool.iota(lane_i[:, :], pattern=[[0, 1]], base=0, channel_multiplier=HALF).then_inc(s_iota, 1)
            pool.memset(w5[:, :], 0.0).then_inc(s_wzero, 1)
            pool.memset(we[:, :], 0.0).then_inc(s_wzero, 1)
            for s in range(2):
                pool.memset(featsT[s][:, :], 1.0).then_inc(s_ones, 1)
                pool.memset(feat[s][:, :], 1.0).then_inc(s_ones, 1)
            pool.memset(ones[:, :], 1.0).then_inc(s_ones, 1)
            pool.wait_ge(s_row_i, 1)
            for i in range(NT):
                pool.indirect_dma_start(out=found[:, i, :], out_offset=None, in_=t["dst"],
                                        in_offset=bass.IndirectOffsetOnAxis(ap=row_i[:, i:i + 1], axis=0)).then_inc(s_found[i // GT], 16)

            def gather(s, r, begun, landed_idx, used_up, dst, table, landed):
                pool.wait_ge(landed_idx[s], 16 * (r + 1))
                wait(pool, used_up[s], r)
                pool.sem_inc(begun, 1)
                for j in range(2 * TILES):
                    pool.indirect_dma_start(out=dst[s][:, j % TILES, j // TILES, :], out_offset=None, in_=table,
                                            in_offset=bass.IndirectOffsetOnAxis(ap=idx[s][:, j:j + 1], axis=0)).then_inc(landed[s], 16)

            pool.wait_ge(s_h24, 16)
            for s in range(2):
                gather(s, 0, s_chunks, idx_in, q2_ready, rows0, d_h24, got_rows)
            pool.wait_ge(s_h3, 16)
            pool.indirect_dma_start(out=fix[:, :], out_offset=None, in_=d_h3,
                                    in_offset=bass.IndirectOffsetOnAxis(ap=mid_i[0:16, 1:2], axis=0)).then_inc(s_fix, 16)
            pool.wait_ge(s_injzero, 16 * 28)
            pool.wait_ge(s_first_i, 1)
            for i in range(NT):
                pool.indirect_dma_start(out=d_inj, out_offset=bass.IndirectOffsetOnAxis(ap=first_i[:, i:i + 1], axis=0),
                                        in_=H[:, i, 3 * C:4 * C], in_offset=None).then_inc(s_inj, 16)
            with pool.Fori(1, CHUNKS // 2) as i:
                for s in range(2):
                    gather(s, i, s_chunks, idx_in, q2_ready, rows0, d_h24, got_rows)
            pool.wait_ge(s_last_i, 1)
            for s in range(2):
                pool.wait_ge(stored[s], 16 * (CHUNKS // 2))
            for i in range(NT):
                pool.indirect_dma_start(out=got0[:, i, :], out_offset=None, in_=d_run0,
                                        in_offset=bass.IndirectOffsetOnAxis(ap=last_i[:, i:i + 1], axis=0)).then_inc(s_got[i // GT], 16)
            pool.wait_ge(s_x1_out, 16 * GROUPS)
            for s in range(2):
                gather(s, 0, s_chunks, idx1_in, z_ready, rows1, d_x1, got1_rows)
            with pool.Fori(1, CHUNKS // 2) as i:
                for s in range(2):
                    gather(s, i, s_chunks, idx1_in, z_ready, rows1, d_x1, got1_rows)
            pool.wait_ge(s_mb_i, 1)
            for s in range(2):
                pool.wait_ge(max_out[s], 16 * (CHUNKS // 2))
            pool.indirect_dma_start(out=max_ab[:, 1:2], out_offset=None, in_=d_max,
                                    in_offset=bass.IndirectOffsetOnAxis(ap=mb_i[:, 0:1], axis=0)).then_inc(s_mb, 16)
            for s in range(2):
                pool.wait_ge(stored1[s], 16 * (CHUNKS // 2))
            for i in range(NT):
                pool.indirect_dma_start(out=H[:, i, 0:2 * C], out_offset=None, in_=d_run1,
                                        in_offset=bass.IndirectOffsetOnAxis(ap=last_i[:, i:i + 1], axis=0)).then_inc(s_got[i // GT], 16)

        @block.scalar
        def _(act):
            act.wait_ge(s_zeros, 1)
            flat = d_inj[0:EP, :].rearrange("(z p r) c -> z p (r c)", z=28, p=P)
            for z in range(28):
                act.dma_start(flat[z], zeros[:, :]).then_inc(s_injzero, 16)
            act.wait_ge(s_half, 1)
            act.wait_ge(s_keys, 32)
            for n, i in enumerate(range(NT_DVE, NT)):
                if n >= 2:
                    act.wait_ge(s_signs, n - 1)
                act.activation(sign[n % 2][:, :], keys[:, :], ACT.Sign, bias=node_half[:, i:i + 1],
                               accum_out=full_rows[:, i:i + 1]).then_inc(s_signs, 1)
            for n in range(3 * NT):
                i, (a, b) = n % NT, W_ORDER[n // NT]
                act.wait_ge(s_proj, n + 1)
                act.activation(H[:, i, a:b], bank[n % 2][0:NP, 0:b - a], ACT.Copy).then_inc(s_sel, 1)

            def exponents(s, r, c):
                act.wait_ge(diff_ready[s], r + 1)
                act.activation(expo[s][:, :, :, :], diff[s][:, :, :, :], ACT.Exp).then_inc(exps_ready[s], 1)

            def widen(s, r, c):
                act.wait_ge(prob_ready[s], r + 1)
                wait(act, probT[s], r)
                act.activation(prob_wide[s][:, :, :, :], prob[s][:, :, :, :].to_broadcast([P, TILES, 2, C]),
                               ACT.Copy).then_inc(wide_ready[s], 1)

            def copies(s, r, c):
                act.wait_ge(keep_in[s], 32 * (r + 1))
                wait(act, run_ready[s], r)
                act.activation(keep_late[s][:, :], keep[s][:, :], ACT.Copy).then_inc(keep_copied[s], 1)
                act.wait_ge(q2_ready[s], r + 1)
                wait(act, msg_ready[s], r)
                act.activation(q2_sb[s][:, :], q2[s], ACT.Copy).then_inc(q2_copied[s], 1)

            def store0(s, r, c):
                act.wait_ge(runT[s], r + 1)
                wait(act, stored[s], 16 * r)
                act.activation(stage0[s][:, :, :].rearrange("p j c -> p (j c)"), p_out0[:, :], ACT.Copy).then_inc(staged[s], 1)
                act.wait_ge(staged[s], r + 1)
                act.dma_start(d_run0[bass.ds(2 * CH * c, 2 * CH), :].rearrange("(p j h) c -> p j (h c)", j=TILES, h=2),
                              stage0[s][:, :, :]).then_inc(stored[s], 16)

            def step0(chunk):
                for work, d in ((exponents, -1), (copies, 0), (widen, -1), (store0, -2)):
                    if chunk(d):
                        work(*chunk(d))

            steps(act, step0, 0, 2)

            def square_and_root(g, first):
                act.wait_ge(s_square, first + g + 1)
                act.activation(sq[:, g * GT:(g + 1) * GT, :], centred[:, g * GT:(g + 1) * GT, :], ACT.Square).then_inc(s_squared, 1)
                act.wait_ge(s_var, first + g + 1)
                act.activation(std[:, g * GT:(g + 1) * GT], var[:, g * GT:(g + 1) * GT], ACT.Sqrt).then_inc(s_sqrt, 1)

            for g in range(GROUPS):
                square_and_root(g, 0)

            def messages(s, r, c):
                act.wait_ge(z_ready[s], r + 1)
                act.activation(relu[s][:, :], p_m[s][:, :], ACT.Relu).then_inc(relu_ready[s], 1)
                act.wait_ge(relu_ready[s], r + 1)
                wait(act, mexp_ready[s], r)
                act.activation(m[s][:, :], relu[s][:, :], ACT.Copy, bias=EPS).then_inc(m_ready[s], 1)

            def decays(s, r, c):
                act.wait_ge(y_ready[s], r + 1)
                act.activation(up[s], y[s][:, :], ACT.Relu).then_inc(updown_ready[s], 1)
                act.activation(down[s][:, :], y[s][:, :], ACT.Relu, scale=-1.0).then_inc(updown_ready[s], 1)
                wait(act, n_run[s], r)
                act.wait_ge(updown_ready[s], 2 * r + 2)
                act.activation(expm[s][:, :], down[s][:, :], ACT.Exp, scale=-1.0).then_inc(expm_ready[s], 1)
                act.activation(decay[s][:, :], up[s], ACT.Exp, scale=-1.0).then_inc(decay_ready[s], 1)

            def store_max(s, r, c):
                act.dma_start(d_max.rearrange("(c e) a -> c (e a)", c=C)[:, bass.ds(c * CH, CH)],
                              runmax[s][C:P, 1:CH + 1]).then_inc(max_out[s], 16)

            def store1(s, r, c):
                act.wait_ge(run1T[s], r + 1)
                wait(act, stored1[s], 16 * r)
                turned = p_out1[s][:, :].rearrange("p (j q h c) -> p j q h c", j=TILES, q=2, h=2)
                for q in range(2):
                    act.activation(stage1[s][:, :, :, q, :], turned[:, :, q], ACT.Copy).then_inc(staged1[s], 1)
                act.wait_ge(staged1[s], 2 * r + 2)
                act.dma_start(d_run1[bass.ds(2 * CH * c, 2 * CH), :].rearrange("(p j h) c -> p (j h c)", j=TILES, h=2),
                              stage1[s][:, :, :, :, :].rearrange("p j h q c -> p (j h q c)")).then_inc(stored1[s], 16)

            def step1(chunk):
                for work, d in ((decays, 0), (store_max, 0), (messages, 1), (store1, -1)):
                    if chunk(d):
                        work(*chunk(d))

            steps(act, step1, 1, 1)

            act.wait_ge(s_dmx, 1)
            act.activation(wgt[:, :, :], dmx[:, :, :], ACT.Exp).then_inc(s_wgt, 1)
            for g in range(GROUPS):
                for i in range(g * GT, (g + 1) * GT):
                    act.wait_ge(s_fT, i + 1)
                    if i >= 2:
                        act.wait_ge(s_y, i - 1)
                    act.activation(featsT[i % 2][0:C, :], bank[i % 2][0:C, 0:NP], ACT.Copy).then_inc(s_fTsb, 1)
                square_and_root(g, GROUPS)

        @block.tensor
        def _(pe):
            pe.wait_ge(s_nodes, 16 * 8)
            pe.wait_ge(s_typed, 2)
            for n in range(3 * NT):
                i, (a, b) = n % NT, W_ORDER[n // NT]
                if n >= 2:
                    pe.wait_ge(s_sel, n - 1)
                for k in range(2):
                    ins = pe.matmul(bank[n % 2][0:NP, 0:b - a], x_typed[k][:, i:N_NODES:NT], w_nodes[:, k, a:b],
                                    start=(k == 0), stop=(k == 1))
                ins.then_inc(s_proj, 1)
            pe.wait_ge(s_ones, 5)
            pe.wait_ge(s_mbcol, 1)
            pe.matmul(bank[2][0:C, 0:1], ones[:, :], mb_col[:, :], start=True, stop=True).then_inc(s_mbps, 1)
            pe.wait_ge(s_const, 16 * 4)
            pe.wait_ge(s_weights, 16 * 10)
            pe.wait_ge(s_mb_i, 1)

            def project0(s, r, c):
                pe.wait_ge(masked[s], r + 1)
                wait(pe, prod_ready[s], r)
                pe.matmul(q4[s], w5[:, :], featm[s][:, :], start=True, stop=True)
                pe.wait_ge(got_rows[s], 16 * 2 * TILES * (r + 1))
                rows = [rows0[s][:, j, :, :].rearrange("p h c -> p (h c)") for j in range(TILES)]
                for j in range(TILES):
                    ins = pe.matmul(q4[s][:, j:CH:TILES], rows[j][:, 1:4 * C:2], ident[:, :], is_transpose=True,
                                    start=False, stop=True, skip_group_check=True)
                ins.then_inc(q4_ready[s], 1)
                wait(pe, q2_copied[s], r)
                pe.matmul(q2[s], w5[:, :], featm[s][:, :], start=True, stop=True)
                for j in range(TILES):
                    ins = pe.matmul(q2[s][:, j:CH:TILES], rows[j][:, 0:4 * C:2], ident[:, :], is_transpose=True,
                                    start=False, stop=True, skip_group_check=True)
                ins.then_inc(q2_ready[s], 1)
                pe.wait_ge(inj_in[s], 16 * (r + 1))
                if isinstance(c, int) and c == 0:
                    pe.wait_ge(s_sel, 3 * NT)
                else:
                    pe.wait_ge(h3_ready[1 - s], r + s)
                for j in range(TILES):
                    ins = pe.matmul(p_inj[:, j:CH:TILES], inj[s][:, j, :], ident[:, :], is_transpose=True,
                                    start=True, stop=True)
                ins.then_inc(injT[s], 1)

            def numerator(s, r, c):
                pe.wait_ge(prod_ready[s], r + 1)
                if not (isinstance(c, int) and c == 0):
                    pe.wait_ge(score_ready[1 - s], r + s)
                for j in range(TILES):
                    ins = pe.matmul(p_num[:, 2 * j:2 * j + 2], prod[s][:, j:CH:TILES], half_sum[:, :], start=True, stop=True)
                ins.then_inc(num_ready[s], 1)

            def turn_prob(s, r, c):
                pe.wait_ge(wide_ready[s], r + 1)
                if not (isinstance(c, int) and c == 0):
                    pe.wait_ge(msg_ready[1 - s], r + s)
                for j in range(TILES):
                    ins = pe.matmul(p_prob[:, j:CH:TILES], prob_wide[s][:, j, :, :].rearrange("p h c -> p (h c)"), ident[:, :],
                                    is_transpose=True, start=True, stop=True)
                ins.then_inc(probT[s], 1)

            def turn_run(s, r, c):
                pe.wait_ge(run_ready[s], r + 1)
                if not (isinstance(c, int) and c == 0):
                    pe.wait_ge(staged[1 - s], r + s)
                for j in range(TILES):
                    ins = pe.matmul(p_out0[:, j * P:(j + 1) * P], run[s][:, j:CH:TILES], ident[:, :], is_transpose=True,
                                    start=True, stop=True)
                ins.then_inc(runT[s], 1)

            def step0(chunk):
                for work, d in ((project0, 1), (numerator, 0), (turn_prob, -1), (turn_run, -2)):
                    if chunk(d):
                        work(*chunk(d))

            steps(pe, step0, 1, 2)

            def project1(s, r, c):
                pe.wait_ge(feat1_in[s], 32 * (r + 1))
                wait(pe, relu_ready[s], r)
                pe.matmul(p_m[s][:, :], we[:, :], feat[s][:, :], start=True, stop=True)
                pe.wait_ge(got1_rows[s], 16 * 2 * TILES * (r + 1))
                for j in range(TILES):
                    ins = pe.matmul(p_m[s][:, j:CH:TILES], rows1[s][:, j, :, :].rearrange("p h c -> p (h c)"), ident[:, :],
                                    is_transpose=True, start=False, stop=True, skip_group_check=True)
                ins.then_inc(z_ready[s], 1)

            def turn1(s, r, c):
                pe.wait_ge(n_run[s], r + 1)
                wait(pe, staged1[s], 2 * r)
                for j in range(TILES):
                    for q, src in enumerate((run_s[s], run_n[s])):
                        ins = pe.matmul(p_out1[s][:, (2 * j + q) * P:(2 * j + q + 1) * P], src[:, j:CH:TILES], ident[:, :],
                                        is_transpose=True, start=True, stop=True)
                ins.then_inc(run1T[s], 1)

            def step1(chunk):
                for work, d in ((project1, 1), (turn1, -1)):
                    if chunk(d):
                        work(*chunk(d))

            steps(pe, step1, 1, 1)

            pe.wait_ge(s_maxwide, 1)
            for b in range(2):
                ins = pe.matmul(bank[2][0:NP, b * C:(b + 1) * C], max_ab_wide[:, b, :], ident[0:C, 0:C],
                                start=True, stop=True)
            ins.then_inc(s_maxps, 1)
            for i in range(NT):
                g = i // GT
                pe.wait_ge(s_feats, g + 1)
                if i >= 2:
                    pe.wait_ge(s_fTsb, i - 1)
                pe.matmul(bank[i % 2][0:C, 0:NP], acc[:, i, :], ident[0:NP, 0:NP], is_transpose=True,
                          start=True, stop=True).then_inc(s_fT, 1)
                if g >= 2:
                    pe.wait_ge(s_square, GROUPS + g - 1)
                at = slice(i % GT * C, (i % GT + 1) * C)
                pe.matmul(wide[g % 2][0:NP, at], ident[0:NP, 0:NP], x1[:, i, :], start=True, stop=True)
                pe.wait_ge(s_fTsb, i + 1)
                pe.matmul(wide[g % 2][0:NP, at], featsT[i % 2][:, :], wm[:, :], start=False, stop=True,
                          skip_group_check=True).then_inc(s_y, 1)

        @block.vector
        def _(dve):
            linked = [0]

            def then(ins):
                linked[0] += 1
                ins.then_inc(s_vec, 1)
                dve.wait_ge(s_vec, linked[0])

            def nodes_of(ap):
                return ap.unsqueeze(2).to_broadcast([NP, ap.shape[1], C])

            def channels_of(ap, tiles=NT):
                return ap.unsqueeze(1).to_broadcast([NP, tiles, C])

            def edge_row(edge):
                then(dve.tensor_scalar(in_row[:, :], edge[:, :], float(HALF), float(1 - 2 * HALF), ALU.is_ge, ALU.mult))
                then(dve.scalar_tensor_tensor(tmp_n[:, :], edge[:, :], 2.0, in_row[:, :], ALU.mult, ALU.add))

            dve.memset(zeros[:, :], 0.0).then_inc(s_zeros, 1)
            dve.wait_ge(s_iota, 2)
            dve.tensor_copy(lane[:, :], lane_i[:, :])
            then(dve.tensor_copy(node[:, :], node_i[:, :]))
            dve.tensor_scalar(node_half[:, :], node[:, :], -1.0, -0.5, ALU.mult, ALU.add).then_inc(s_half, 1)
            then(dve.memset(xT[C:C + 1], 1.0))
            dve.wait_ge(s_nodes, 16 * 8)
            for k in range(2):
                dve.scalar_tensor_tensor(x_typed[k], ntype_i[:, :], float(k), xT, ALU.is_equal, ALU.mult).then_inc(s_typed, 1)
            dve.wait_ge(s_keys, 32)
            for i in range(NT_DVE):
                ins = dve.tensor_scalar(le[i % 4][:, :], keys[:, :], node[:, i:i + 1], 0.0, ALU.is_le, ALU.add,
                                        accum_out=full_rows[:, i:i + 1])
                if i % 4 == 3:
                    then(ins)
            then(dve.memset(mb_col[:, :], 0.0))
            dve.wait_ge(s_signs, NT - NT_DVE)
            then(dve.tensor_scalar(full_rows[:, NT_DVE:NT], full_rows[:, NT_DVE:NT], -0.5, ROWS / 2, ALU.mult, ALU.add))
            dve.tensor_copy(row_i[:, :], full_rows[:, :]).then_inc(s_row_i, 1)
            then(dve.memset(start[:, :], 0.0))
            dve.wait_ge(s_edges, 48)
            dve.tensor_tensor(keep_r[:, :], dst_i[:, :], prev_i[:, :], ALU.is_equal).then_inc(s_rowlists, 1)
            then(dve.tensor_tensor(dst_step[:, :], prev_i[:, :], dst_i[:, :], ALU.subtract))
            dve.tensor_scalar(pen_r[:, :], dst_step[:, :], BIG, None, ALU.mult).then_inc(s_rowlists, 1)
            dve.tensor_copy(type_r[:, :], type_i[:, :]).then_inc(s_rowlists, 1)
            then(dve.tensor_copy(mid[:, :], mid_i[:, :]))
            then(dve.tensor_tensor(mid_same[:, :], mid[:, 0:1], mid[:, 1:2], ALU.is_equal))
            then(dve.tensor_scalar(cross[:, :], node[:, :], mid[:, 1:2], mid_same[:, :], ALU.is_equal, ALU.mult))
            then(dve.tensor_scalar(not_cross[:, :], cross[:, :], -1.0, 1.0, ALU.mult, ALU.add))
            for i in range(NT):
                dve.wait_ge(s_found[i // GT], 16 * GT)
                ins = dve.tensor_scalar(le[i % 4][:, 0:ROW], found[:, i, :], node[:, i:i + 1], 0.0, ALU.is_le, ALU.add,
                                        accum_out=in_row[:, i:i + 1])
                if i % 4 == 3 or i == NT - 1:
                    then(ins)
            dve.scalar_tensor_tensor(end[:, :], full_rows[:, :], float(ROW), in_row[:, :], ALU.mult, ALU.add).then_inc(s_end, 1)
            dve.wait_ge(s_end, 1)
            then(dve.tensor_copy(start[:, 1:NT], end[:, 0:NT - 1]))
            then(dve.tensor_scalar(last[:, :], end[:, :], -1.0, 0.0, ALU.add, ALU.max))
            edge_row(last)
            dve.tensor_copy(last_i[:, :], tmp_n[:, :]).then_inc(s_last_i, 1)
            dve.wait_ge(s_last_i, 1)
            then(dve.scalar_tensor_tensor(tmp_n[:, :], last[:, :], float(-HALF), cross[:, :], ALU.add, ALU.mult))
            dve.tensor_reduce(mb_col[:, :], tmp_n[:, :], AX.X, ALU.add).then_inc(s_mbcol, 1)
            dve.wait_ge(s_mbcol, 1)
            dve.wait_ge(s_shift, 16)
            then(dve.tensor_tensor(has_edges[:, :], end[:, :], start[:, :], ALU.is_gt))
            edge_row(start)
            then(dve.tensor_tensor(tmp_n[:, :], tmp_n[:, :], has_edges[:, :], ALU.mult))
            then(dve.tensor_scalar(in_row[:, :], has_edges[:, :], -1.0, 1.0, ALU.mult, ALU.add))
            then(dve.scalar_tensor_tensor(in_row[:, :], node[:, :], float(DUMP), in_row[:, :], ALU.add, ALU.mult))
            then(dve.tensor_tensor(tmp_n[:, :], tmp_n[:, :], in_row[:, :], ALU.add))
            dve.tensor_copy(first_i[:, :], tmp_n[:, :]).then_inc(s_first_i, 1)
            dve.wait_ge(s_mbps, 1)
            dve.tensor_tensor(mb_i[:, :], bank[2][0:C, 0:1], lane[:, :], ALU.add).then_inc(s_mb_i, 1)

            for s in range(2):
                dve.memset(h3d[s][:, :], 0.0)
                then(dve.memset(run[s][:, :], 0.0))
            dve.wait_ge(s_const, 16 * 4)

            def score_parts(s, r, c):
                dve.wait_ge(num_ready[s], r + 1)
                dve.tensor_scalar(score[s][:, :, :, :].rearrange("p j h a -> p (j h a)"), p_num[:, 0:2 * TILES], 0.25, None,
                                  ALU.mult).then_inc(score_ready[s], 1)
                dve.wait_ge(score_ready[s], r + 1)
                dve.tensor_reduce(top[s][:, :, :], score[s][:, :, :, :], AX.X, ALU.max).then_inc(softmax_step[s], 1)
                dve.wait_ge(softmax_step[s], 3 * r + 1)
                wait(dve, exps_ready[s], r)
                dve.tensor_tensor(diff[s][:, :, :, :], score[s][:, :, :, :], top[s][:, :, :].unsqueeze(3), ALU.subtract).then_inc(diff_ready[s], 1)

            def mask(s, r, c):
                dve.wait_ge(feat_in[s], 16 * 4 * (r + 1))
                wait(dve, q2_ready[s], r)
                dve.scalar_tensor_tensor(featm[s][:, :], types[s][:, :], type_of_row[:, :], feat[s][:, :],
                                         ALU.is_equal, ALU.mult).then_inc(masked[s], 1)

            def products(s, r, c):
                dve.wait_ge(keep_in[s], 32 * (r + 1))
                dve.wait_ge(injT[s], r + 1)
                if not (isinstance(c, int) and c == 0):
                    dve.wait_ge(h3_ready[1 - s], r + s)
                dve.tensor_tensor_scan(h3d[s][:, :], keep[s][:, :], p_inj[:, :], h3d[1 - s][:, CH - 1:CH],
                                       ALU.mult, ALU.add).then_inc(h3_ready[s], 1)
                dve.wait_ge(h3_ready[s], r + 1)
                dve.wait_ge(q4_ready[s], r + 1)
                wait(dve, num_ready[s], r)
                dve.tensor_tensor(prod[s][:, :], h3d[s][:, :], q4[s], ALU.mult).then_inc(prod_ready[s], 1)

            def probabilities(s, r, c):
                dve.wait_ge(exps_ready[s], r + 1)
                dve.tensor_reduce(total[s][:, :, :], expo[s][:, :, :, :], AX.X, ALU.add).then_inc(softmax_step[s], 1)
                dve.wait_ge(softmax_step[s], 3 * r + 2)
                dve.reciprocal(inv[s][:, :, :], total[s][:, :, :]).then_inc(softmax_step[s], 1)
                dve.wait_ge(softmax_step[s], 3 * r + 3)
                wait(dve, wide_ready[s], r)
                dve.tensor_tensor(prob[s][:, :, :, :], expo[s][:, :, :, :], inv[s][:, :, :].unsqueeze(3), ALU.mult).then_inc(prob_ready[s], 1)

            def message_sums(s, r, c):
                dve.wait_ge(probT[s], r + 1)
                dve.wait_ge(q2_copied[s], r + 1)
                dve.tensor_tensor(msg[s][:, :], p_prob[:, :], q2_sb[s][:, :], ALU.mult).then_inc(msg_ready[s], 1)
                dve.wait_ge(msg_ready[s], r + 1)
                dve.wait_ge(keep_copied[s], r + 1)
                if not (isinstance(c, int) and c == 0):
                    dve.wait_ge(run_ready[1 - s], r + s)
                wait(dve, runT[s], r)
                dve.tensor_tensor_scan(run[s][:, :], keep_late[s][:, :], msg[s][:, :], run[1 - s][:, CH - 1:CH],
                                       ALU.mult, ALU.add).then_inc(run_ready[s], 1)

            def step0(chunk):
                for work, d in ((score_parts, -1), (mask, 1), (products, 0), (probabilities, -1), (message_sums, -2)):
                    if chunk(d):
                        work(*chunk(d))

            steps(dve, step0, 1, 2)

            def layer_norm(src, g, first):
                at = slice(g * GT, (g + 1) * GT)
                then(dve.tensor_reduce(mean[:, at], src, AX.X, ALU.add))
                then(dve.tensor_scalar(mean[:, at], mean[:, at], 1.0 / C, None, ALU.mult))
                dve.tensor_tensor(centred[:, at, :], src, nodes_of(mean[:, at]), ALU.subtract).then_inc(s_square, 1)
                dve.wait_ge(s_squared, first + g + 1)
                then(dve.tensor_reduce(var[:, at], sq[:, at, :], AX.X, ALU.add))
                dve.tensor_scalar(var[:, at], var[:, at], 1.0 / C, LN_EPS, ALU.mult, ALU.add).then_inc(s_var, 1)
                dve.wait_ge(s_sqrt, first + g + 1)
                then(dve.reciprocal(rstd[:, at], std[:, at]))
                return dve.tensor_tensor(x1[:, at, :], centred[:, at, :], nodes_of(rstd[:, at]), ALU.mult)

            for s in range(2):
                dve.memset(feat[s][:, :], 1.0)
                dve.memset(run_s[s][:, :], 0.0)
                dve.memset(run_n[s][:, :], 0.0)
                then(dve.memset(runmax[s][:, :], 0.0))
            dve.wait_ge(s_sel, 3 * NT)
            then(dve.tensor_tensor(acc[:, :, :], x_sb[:, :, :], H[:, :, 0:C], ALU.add))
            dve.wait_ge(s_cut0, 16)
            then(dve.tensor_tensor(across, channels_of(cut0[:, :]), nodes_of(cross[:, :]), ALU.mult))
            dve.tensor_tensor(acc[:, :, :], acc[:, :, :], across, ALU.add).then_inc(s_ones1, 1)
            dve.wait_ge(s_ones1, 1)
            for g in range(GROUPS):
                at = slice(g * GT, (g + 1) * GT)
                dve.wait_ge(s_got[g], 16 * GT)
                then(dve.tensor_tensor(got0[:, at, :], got0[:, at, :], nodes_of(has_edges[:, at]), ALU.mult))
                then(dve.tensor_tensor(acc[:, at, :], acc[:, at, :], got0[:, at, :], ALU.add))
                layer_norm(acc[:, at, :], g, 0).then_inc(s_x1, 1)
            dve.wait_ge(s_x1, GROUPS)

            def maxima(s, r, c):
                first = isinstance(c, int) and c == 0
                wait(dve, max_out[s], 16 * r)
                if not first:
                    dve.wait_ge(max_ready[1 - s], 2 * (r + s))
                dve.tensor_copy(runmax[s][:, 0:1], runmax[1 - s][:, CH:CH + 1]).then_inc(max_ready[s], 1)
                dve.wait_ge(pen_in[s], 32 * (r + 1))
                dve.wait_ge(m_ready[s], r + 1)
                dve.tensor_tensor_scan(runmax[s][:, 1:CH + 1], keep[s][:, :], m[s][:, :], runmax[1 - s][:, CH:CH + 1],
                                       ALU.add, ALU.max).then_inc(max_ready[s], 1)
                dve.wait_ge(max_ready[s], 2 * r + 2)
                wait(dve, updown_ready[s], 2 * r)
                dve.tensor_tensor(y[s][:, :], runmax[s][:, 0:CH], keep[s][:, :], ALU.add).then_inc(shift_ready[s], 1)
                dve.wait_ge(shift_ready[s], r + 1)
                dve.tensor_tensor(y[s][:, :], m[s][:, :], y[s][:, :], ALU.subtract).then_inc(y_ready[s], 1)

            def sums(s, r, c):
                first = isinstance(c, int) and c == 0
                dve.wait_ge(expm_ready[s], r + 1)
                dve.tensor_tensor(mexp[s][:, :], m[s][:, :], expm[s][:, :], ALU.mult).then_inc(mexp_ready[s], 1)
                dve.wait_ge(decay_ready[s], r + 1)
                wait(dve, run1T[s], r)
                if not first:
                    dve.wait_ge(s_run[1 - s], r + s)
                dve.tensor_tensor_scan(run_s[s][:, :], decay[s][:, :], expm[s][:, :], run_s[1 - s][:, CH - 1:CH],
                                       ALU.mult, ALU.add).then_inc(s_run[s], 1)
                dve.wait_ge(mexp_ready[s], r + 1)
                if not first:
                    dve.wait_ge(n_run[1 - s], r + s)
                dve.tensor_tensor_scan(run_n[s][:, :], decay[s][:, :], mexp[s][:, :], run_n[1 - s][:, CH - 1:CH],
                                       ALU.mult, ALU.add).then_inc(n_run[s], 1)

            def step1(chunk):
                for work, d in ((maxima, 0), (sums, -1)):
                    if chunk(d):
                        work(*chunk(d))

            steps(dve, step1, 0, 1)

            dve.wait_ge(s_mb, 16)
            then(dve.tensor_copy(max_ab[:, 0:1], runmax[1][0:C, CH:CH + 1]))
            dve.tensor_copy(max_ab_wide[:, :, :], max_ab[:, :].unsqueeze(2).to_broadcast([C, 2, NP])).then_inc(s_maxwide, 1)
            dve.wait_ge(s_maxps, 1)
            then(dve.tensor_copy(mx[:, :, :], bank[2][0:NP, 0:2 * C].rearrange("p (q c) -> p q c", q=2)))
            then(dve.tensor_tensor(mm[:, :], mx[:, 0, :], mx[:, 1, :], ALU.max))
            dve.tensor_tensor(dmx[:, :, :], mx[:, :, :], mm[:, :].unsqueeze(1).to_broadcast([NP, 2, C]), ALU.subtract).then_inc(s_dmx, 1)
            dve.wait_ge(s_wgt, 1)
            dve.wait_ge(s_cut1, 16)
            then(dve.tensor_tensor(late[:, :, 0, :], channels_of(wgt[:, 1, :]), nodes_of(cross[:, :]), ALU.mult))
            then(dve.tensor_tensor(late[:, :, 0, :], late[:, :, 0, :], nodes_of(not_cross[:, :]), ALU.add))
            then(dve.tensor_tensor(late[:, :, 1, :], late[:, :, 0, :], nodes_of(has_edges[:, :]), ALU.mult))
            then(dve.tensor_tensor(cut1[:, :, :], cut1[:, :, :], wgt[:, 0:1, :].to_broadcast([NP, 2, C]), ALU.mult))
            for q in range(2):
                then(dve.tensor_tensor(far_part[:, :, q, :], channels_of(cut1[:, q, :]), nodes_of(cross[:, :]), ALU.mult))

            def features_of(g):
                at = slice(g * GT, (g + 1) * GT)
                dve.wait_ge(s_got[g], 2 * 16 * GT)
                then(dve.tensor_tensor(got1[:, at, :, :], got1[:, at, :, :], late[:, at, :, :], ALU.mult))
                then(dve.tensor_tensor(got1[:, at, :, :], got1[:, at, :, :], far_part[:, at, :, :], ALU.add))
                then(dve.reciprocal(acc[:, at, :], got1[:, at, 0, :]))
                then(dve.tensor_tensor(acc[:, at, :], got1[:, at, 1, :], acc[:, at, :], ALU.mult))
                dve.tensor_tensor(acc[:, at, :], x1[:, at, :], acc[:, at, :], ALU.add).then_inc(s_feats, 1)

            def normalised(g):
                dve.wait_ge(s_y, (g + 1) * GT)
                ins = layer_norm(wide[g % 2][0:NP, 0:GT * C].rearrange("p (i c) -> p i c", c=C), g, GROUPS)
                ins.then_inc(s_fin, 1)

            for g in range(GROUPS):
                features_of(g)
                if g >= 1:
                    normalised(g - 1)
            normalised(GROUPS - 1)


def kernel(x, src, dst, edge_attr_16, edge_attr_32, edge_type_3, node_type_2,
           L0_gnn_W1, L0_gnn_b1, L0_gnn_W2, L0_gnn_b2, L0_gnn_W3, L0_gnn_b3, L0_gnn_W4, L0_gnn_b4,
           L0_gnn_W5, L0_gnn_b5, L1_gnn_We, L1_gnn_be, L1_gnn_Wm, L1_gnn_bm):
    import numpy as np
    import concourse.bacc as bacc
    from concourse.bass_utils import run_bass_kernel_spmd as run

    def padded(a, value):
        return np.concatenate([np.asarray(a), np.full(EP - N_EDGES, value, np.int32)])

    def features(a):
        a = np.asarray(a).T
        return np.concatenate([a, np.zeros((a.shape[0], EP - N_EDGES), a.dtype)], axis=1)

    dst_p = padded(dst, N_NODES)
    src_p = padded(src, 0)
    row = np.arange(P) % C
    type_of_row = np.where(row < T_EDGE * F0, row // F0, np.where(row < T_EDGE * (F0 + 1), row - T_EDGE * F0, -1))
    arrays = {
        "x": x, "xT": np.asarray(x).T,
        "src": src_p.reshape(2, CHUNKS, P, TILES).transpose(1, 2, 0, 3).reshape(CHUNKS * P, 2 * TILES),
        "dst": dst_p.reshape(ROWS, ROW),
        "dst_prev": np.concatenate([np.full(1, -1, np.int32), dst_p[:-1]]).reshape(P, PER_P),
        "keys": dst_p[ROW - 1::ROW].reshape(1, ROWS),
        "mid": dst_p[HALF - 1:HALF + 1].reshape(1, 2),
        "etype": padded(edge_type_3, 0).reshape(P, PER_P),
        "node_type": np.asarray(node_type_2).reshape(1, N_NODES),
        "ea16x3T": np.concatenate([features(edge_attr_16)] * T_EDGE), "ea32T": features(edge_attr_32),
        "W1": L0_gnn_W1, "b1": L0_gnn_b1, "W3": L0_gnn_W3, "b3": L0_gnn_b3,
        "W24": np.stack([L0_gnn_W2, L0_gnn_W4], axis=-1).reshape(2, C, 2 * C),
        "b24": np.stack([L0_gnn_b2, L0_gnn_b4], axis=-1).reshape(2, 2 * C),
        "W5": L0_gnn_W5, "b5": L0_gnn_b5,
        "We": L1_gnn_We, "be": np.asarray(L1_gnn_be).reshape(1, C),
        "Wm": L1_gnn_Wm, "bm": np.asarray(L1_gnn_bm).reshape(1, C),
        "ident": np.eye(P, dtype=np.float32),
        "half_sum": np.kron(np.eye(2), np.ones((C, 1))).astype(np.float32),
        "type_of_row": type_of_row.astype(np.float32).reshape(P, 1),
    }
    nc = bacc.Bacc("TRN2", target_bir_lowering=False, num_devices=1)
    feed, aps = {}, {}
    for name, a in arrays.items():
        a = np.ascontiguousarray(a)
        feed[f"in_{name}"] = a
        aps[name] = nc.dram_tensor(f"in_{name}", a.shape, mybir.dt.from_np(a.dtype), kind="ExternalInput").ap()
    out = nc.dram_tensor("out", (N_NODES, C), mybir.dt.float32, kind="ExternalOutput").ap()
    gnn_program(nc, aps, out)
    return run(nc, [feed], core_ids=[0]).results[0]["out"]
```
